# Optimizing a Trainium2 kernel written in Bass

```python
import numpy as np
import jax
import jax.numpy as jnp

def _softmax(x, axis=-1):
    return jax.nn.softmax(x, axis=axis)

def _gelu(x):
    return jax.nn.gelu(x, approximate=True)

def _silu(x):
    return jax.nn.silu(x)

def _sigmoid(x):
    return jax.nn.sigmoid(x)

def _layernorm(x, axis=-1, eps=1e-05):
    m = jnp.mean(x, axis=axis, keepdims=True)
    v = jnp.var(x, axis=axis, keepdims=True)
    return (x - m) / jnp.sqrt(v + eps)

def _scatter_add(tgt, idx, src, axis=0):
    return tgt.at[idx].add(src)

def _segment_sum(src, seg, n):
    return jax.ops.segment_sum(src, seg, n)
kernel_name = 'mk_seq_postln_d1_jaxref_r8_dfd1be'

def setup_inputs(seed: int=0):
    np.random.seed(seed)
    _w = jnp.asarray

    def _L0_attn_setup():
        import jax, jax.numpy as jnp
        import numpy as np
        EPS = 1e-06

        def _rmsnorm(x, w):
            ms = jnp.mean(jnp.square(x), axis=-1, keepdims=True)
            return x * jax.lax.rsqrt(ms + EPS) * w
        key = jax.random.key(seed)
        k1, k2, k3 = jax.random.split(key, 3)
        B, T, D = (4, 512, 128)
        d_inner = D
        x = jax.random.normal(k1, (B, T, D), dtype=jnp.float32)
        w_norm = jnp.ones((D,), dtype=jnp.float32)
        W_in = jax.random.normal(k2, (D, 3 * d_inner), dtype=jnp.float32) / np.sqrt(D)
        lambda_log = jnp.full((d_inner,), -0.5, dtype=jnp.float32)
        W_out = jax.random.normal(k3, (d_inner, D), dtype=jnp.float32) / np.sqrt(d_inner)
        return {'x': x, 'w_norm': w_norm, 'W_in': W_in, 'lambda_log': lambda_log, 'W_out': W_out}
    _L0_attn_in = _L0_attn_setup()

    def _L0_ffn_setup():
        import jax, jax.numpy as jnp
        import numpy as np
        HIDDEN = 128
        INTER = 256
        NUM_EXPERTS = 8
        TOPK = 2
        STD = 0.02
        key = jax.random.key(seed)
        k1, k2, k3, k4 = jax.random.split(key, 4)
        return {'hidden_states': jax.random.normal(k1, (1, 256, HIDDEN), dtype=jnp.float32), 'w1': jax.random.normal(k2, (NUM_EXPERTS, 2 * INTER, HIDDEN), dtype=jnp.float32) * STD, 'w2': jax.random.normal(k3, (NUM_EXPERTS, HIDDEN, INTER), dtype=jnp.float32) * STD, 'router_w': jax.random.normal(k4, (NUM_EXPERTS, HIDDEN), dtype=jnp.float32) * STD}
    _L0_ffn_in = _L0_ffn_setup()
    _d = {'L0_attn_x': _L0_attn_in['x'], 'L0_attn_w_norm': _L0_attn_in['w_norm'], 'L0_attn_W_in': _L0_attn_in['W_in'], 'L0_attn_lambda_log': _L0_attn_in['lambda_log'], 'L0_attn_W_out': _L0_attn_in['W_out'], 'L0_ffn_w1': _L0_ffn_in['w1'], 'L0_ffn_w2': _L0_ffn_in['w2'], 'L0_ffn_router_w': _L0_ffn_in['router_w']}
    _x0 = _d['L0_attn_x']
    _d['L0_attn_x'] = jax.random.normal(jax.random.fold_in(jax.random.key(seed), 1), (8, 1024, 128), dtype=_x0.dtype)
    del _x0
    return _d

def reference(L0_attn_x, L0_attn_w_norm, L0_attn_W_in, L0_attn_lambda_log, L0_attn_W_out, L0_ffn_w1, L0_ffn_w2, L0_ffn_router_w):

    def _L0_attn_ref(x, w_norm, W_in, lambda_log, W_out):
        import jax, jax.numpy as jnp
        import numpy as np
        EPS = 1e-06

        def _rmsnorm(x, w):
            ms = jnp.mean(jnp.square(x), axis=-1, keepdims=True)
            return x * jax.lax.rsqrt(ms + EPS) * w
        B, T, D = x.shape
        residual = x
        x_norm = _rmsnorm(x, w_norm)
        proj = jnp.einsum('btd,de->bte', x_norm, W_in)
        gate_a, gate_r, v = jnp.split(proj, 3, axis=-1)
        a = jax.nn.sigmoid(gate_a)
        r = jax.nn.sigmoid(gate_r)
        v = jax.nn.gelu(v, approximate=False)
        lam = jax.nn.sigmoid(lambda_log)
        u = (1.0 - a) * (r * v) * lam
        a_t = jnp.swapaxes(a, 0, 1)
        u_t = jnp.swapaxes(u, 0, 1)

        def step(h, au):
            at, ut = au
            h = at * h + ut
            return (h, h)
        h0 = jnp.zeros((B, a.shape[-1]), dtype=x.dtype)
        _, ys = jax.lax.scan(step, h0, (a_t, u_t))
        y = jnp.swapaxes(ys, 0, 1)
        return residual + jnp.einsum('bte,ed->btd', y, W_out)

    def _L0_ffn_ref(hidden_states, w1, w2, router_w):
        import jax, jax.numpy as jnp
        import numpy as np
        HIDDEN = 128
        INTER = 256
        NUM_EXPERTS = 8
        TOPK = 2
        STD = 0.02
        orig_shape = hidden_states.shape
        dtype = hidden_states.dtype
        x = hidden_states.reshape(-1, orig_shape[-1])
        E = w1.shape[0]
        gating = x @ router_w.T
        probs = jax.nn.softmax(gating.astype(jnp.float32), axis=-1)
        topk_w, sel = jax.lax.top_k(probs, TOPK)
        topk_w = topk_w.astype(dtype)
        combine = (jax.nn.one_hot(sel, E, dtype=dtype) * topk_w[..., None]).sum(axis=1)
        h = jnp.einsum('td,eid->tei', x, w1)
        gate = jax.nn.silu(h[..., :INTER])
        y = h[..., INTER:] * gate
        out = jnp.einsum('tei,ehi,te->th', y, w2, combine)
        return out.reshape(orig_shape)
    x = L0_attn_x
    x = _layernorm(x + _L0_attn_ref(x, L0_attn_w_norm, L0_attn_W_in, L0_attn_lambda_log, L0_attn_W_out), axis=-1)
    x = _layernorm(x + _L0_ffn_ref(x, L0_ffn_w1, L0_ffn_w2, L0_ffn_router_w), axis=-1)
    return x

_drawn_inputs = setup_inputs


def setup_inputs(seed=0):
    import zlib

    import numpy as np

    out = dict(_drawn_inputs(seed))
    spreads = {'L0_attn_w_norm': (1.0, 0.6), 'L0_attn_lambda_log': (-0.5, 0.6)}
    factors = {'L0_ffn_w1': 8.0, 'L0_ffn_w2': 8.0, 'L0_ffn_router_w': 8.0}
    for name, (base, spread) in spreads.items():
        noise = np.random.default_rng([zlib.crc32(name.encode()), seed]).standard_normal(out[name].shape)
        drawn = base * np.exp(spread * noise) if base else spread * noise
        out[name] = jnp.asarray(drawn.astype(out[name].dtype))
    for name, factor in factors.items():
        out[name] = (out[name] * factor).astype(out[name].dtype)
    return out
```

```python
import concourse.bass as bass
from concourse import mybir
from contextlib import ExitStack

F32 = mybir.dt.float32
BF16 = mybir.dt.bfloat16
I32 = mybir.dt.int32
ALU = mybir.AluOpType
ACT = mybir.ActivationFunctionType
AX = mybir.AxisListType

P = 128
D = 128
E = 8
INTER = 256
TOKENS = 8 * 1024
CHUNK = 2048
CHUNKS = TOKENS // CHUNK
TILES = CHUNK // P
GROUP = 512
GROUPS = CHUNK // GROUP
TPG = GROUP // P
SEQ_GROUPS = 1024 // GROUP
MAX_BLOCKS = 2 * TILES + E
RING = 4
RMS_EPS = 1e-6
LN_EPS = 1e-5
LOWEST = -3.0e38
RSQRT_MAGIC = float(0x5F3759DF)


def moe_layer(nc, x, w_norm, w_in, lambda_log, w_out, w1, w2, router_w, out):
    x_rows = x.rearrange("b t d -> (b t) d")
    out_rows = out.rearrange("b t d -> (b t) d")

    def chunk_view(rows, c):
        return rows[c * CHUNK:(c + 1) * CHUNK, :].rearrange("(g p j) d -> p g (j d)", p=P, j=TPG)

    def group_view(rows, c, g):
        r0 = c * CHUNK + g * GROUP
        return rows[r0:r0 + GROUP, :].rearrange("(p j) d -> p (j d)", j=TPG)

    x1_dram = [nc.dram_tensor(f"x1_rows_{c}", [CHUNK, D], F32, kind="Internal").ap() for c in range(CHUNKS)]
    slot_dram = [nc.dram_tensor(f"slot_rows_{c}", [MAX_BLOCKS * P, D], F32, kind="Internal").ap()
                 for c in range(CHUNKS)]

    with ExitStack() as ctx:
        def sb(name, shape, dt=F32):
            return ctx.enter_context(nc.sbuf_tensor(name, shape, dt))

        def bank(name):
            return ctx.enter_context(nc.psum_tensor(name, [P, 512], F32))

        def sem(name):
            return ctx.enter_context(nc.semaphore(name))

        w_in_raw = sb("w_in_raw", [P, 3 * D])
        w_in_sb = sb("w_in_sb", [P, 3 * D])
        w_out_sb = sb("w_out_sb", [P, D])
        w_norm_sb = sb("w_norm_sb", [P, 1])
        lam_log = sb("lam_log", [P, 1])
        lam = sb("lam", [P, 1])
        w_out_raw = sb("w_out_raw", [P, D])
        router_t = sb("router_t", [P, E])
        w1_raw = sb("w1_raw", [P, E * 4, P])
        w2_raw = sb("w2_raw", [P, E * 2, P])
        w1_t = sb("w1_t", [P, E * 2 * INTER])
        w2_t = sb("w2_t", [P, 2, E * D])
        ident = sb("ident", [P, P])
        before = sb("before", [P, P], BF16)
        ones = sb("ones", [P, P], BF16)
        lane_iota = sb("lane_iota", [P, P], BF16)
        block_iota = sb("block_iota", [P, 3, MAX_BLOCKS], BF16)
        token_parts = sb("token_parts", [P, TILES, 3, MAX_BLOCKS], BF16)
        first_key = sb("first_key", [P, TILES, E])
        block_no = sb("block_no", [P, MAX_BLOCKS, E])

        x_in = sb("x_in", [P, 2, TILES, D])
        square_junk = sb("square_junk", [P, TILES, D])
        sumsq = sb("sumsq", [P, TILES])
        rms_inv = sb("rms_inv", [P, TILES])
        nr_half = sb("nr_half", [P, TILES])
        nr_tmp = sb("nr_tmp", [P, TILES])
        nr_int = sb("nr_int", [P, TILES], I32)
        x_norm = sb("x_norm", [P, 2, GROUP])
        x_norm_t = sb("x_norm_t", [P, 2, GROUP])
        tanh_a = sb("tanh_a", [P, 2, GROUP])
        tanh_r = sb("tanh_r", [P, 2, GROUP])
        gelu_v = sb("gelu_v", [P, 2, GROUP])
        gate_a = sb("gate_a", [P, GROUP])
        u1 = sb("u1", [P, GROUP])
        u2 = sb("u2", [P, GROUP])
        state = sb("state", [P, 2, GROUP])
        z = sb("z", [P, TILES, D])
        stats = sb("stats", [P, TILES, 6])
        mean = sb("mean", [P, TILES])
        mean_diff = sb("mean_diff", [P, TILES])
        var = sb("var", [P, TILES])
        rstd = sb("rstd", [P, TILES])
        neg_mean_rstd = sb("neg_mean_rstd", [P, TILES])
        x1 = [sb(f"x1_{k}", [P, TILES, D]) for k in range(3)]
        x1_t = sb("x1_t", [P, 2, GROUP])

        logits = sb("logits", [P, TILES, E])
        top1 = sb("top1", [P, TILES])
        top2 = sb("top2", [P, TILES])
        top_gap = [sb(f"top_gap_{k}", [P, TILES]) for k in range(2)]
        route_a = sb("route_a", [P, TILES, E])
        route_b = sb("route_b", [P, TILES])
        pick = sb("pick", [P, 2, TILES, E])
        picked = sb("picked", [P, TILES + 1, E], BF16)
        shifted = [sb(f"shifted_{k}", [P, TILES, E]) for k in range(2)]
        exp_logits = [sb(f"exp_logits_{k}", [P, TILES, E]) for k in range(3)]
        exp_gap = [sb(f"exp_gap_{k}", [P, TILES]) for k in range(3)]
        weight = sb("weight", [P, 2, TILES])
        count_i = sb("count_i", [P, E], I32)
        blocks_of = sb("blocks_of", [P, E])
        block_end = sb("block_end", [P, E])
        slot_base = sb("slot_base", [P, E])
        one_row = sb("one_row", [P, E])
        slot_f = sb("slot_f", [P, 2, TILES])
        slot_i = [sb(f"slot_i_{k}", [P, 2, TILES], I32) for k in range(3)]
        part_i = sb("part_i", [P, 2, 2 * TILES], I32)
        slot_block = sb("slot_block", [P, 2 * TILES])
        slot_lane = sb("slot_lane", [P, 2 * TILES])
        ended = sb("ended", [P, MAX_BLOCKS, E])
        expert_f = sb("expert_f", [P, MAX_BLOCKS])
        w1_at = [sb(f"w1_at_{k}", [P, MAX_BLOCKS], I32) for k in range(2)]
        w2_at = [sb(f"w2_at_{k}", [P, MAX_BLOCKS], I32) for k in range(2)]
        lane_hot = sb("lane_hot", [P, 2, P], BF16)
        block_hot = sb("block_hot", [P, 2, 3, MAX_BLOCKS], BF16)
        token_pj = sb("token_pj", [P, MAX_BLOCKS])
        token_ps = sb("token_ps", [P, 3, MAX_BLOCKS])
        token_of = [sb(f"token_of_{k}", [P, MAX_BLOCKS], I32) for k in range(2)]

        xg = [sb(f"xg_{k}", [P, D]) for k in range(RING)]
        xg_t = sb("xg_t", [P, 2, P])
        silu = sb("silu", [P, 2, INTER])
        y = sb("y", [P, 2, INTER])
        y_t = sb("y_t", [P, 2, INTER])
        rows_out = sb("rows_out", [P, RING, D])

        og = sb("og", [P, 2, TILES, D])
        s = sb("s", [P, TILES, D])
        half_s = sb("half_s", [P, 2, D])
        fin = sb("fin", [P, TILES, D])

        ps_t = bank("ps_t")
        ps_a = bank("ps_a")
        ps_r = bank("ps_r")
        ps_v = bank("ps_v")
        ps_o = bank("ps_o")
        ps_y = bank("ps_y")
        ps_u = bank("ps_u")
        ps_q = bank("ps_q")
        ps_h = [ps_a, ps_r]
        ps_x = ps_v
        ps_logits = ps_q[:, 0:TILES * E].rearrange("p (i e) -> p i e", e=E)
        ps_rank = ps_q[:, 0:(TILES + 1) * E].rearrange("p (i e) -> p i e", e=E)
        ps_token = ps_q[:, 0:3 * MAX_BLOCKS].rearrange("p (a b) -> p a b", a=3)

        w_ready = sem("w_ready")
        experts_in = sem("experts_in")
        consts_ready = sem("consts_ready")
        consts_step = sem("consts_step")
        lam_ready = sem("lam_ready")
        x_loaded = [sem(f"x_loaded_{k}") for k in range(2)]
        sumsq_ready = sem("sumsq_ready")
        xn_ready = sem("xn_ready")
        xn_turned = sem("xn_turned")
        xn_t_ready = sem("xn_t_ready")
        proj_ready = sem("proj_ready")
        gates_ready = sem("gates_ready")
        state_ready = sem("state_ready")
        mixed = sem("mixed")
        z_ready = sem("z_ready")
        x1_ready = sem("x1_ready")
        x1_stored = [sem(f"x1_stored_{c}") for c in range(CHUNKS)]
        x1_turned = sem("x1_turned")
        x1_t_ready = sem("x1_t_ready")
        logits_done = sem("logits_done")
        shifted_ready = sem("shifted_ready")
        exps_ready = sem("exps_ready")
        picked_ready = sem("picked_ready")
        rank_ready = sem("rank_ready")
        experts_known = sem("experts_known")
        hot_ready = sem("hot_ready")
        hot_used = sem("hot_used")
        token_sum = sem("token_sum")
        tokens_known = sem("tokens_known")
        w_turned = sem("w_turned")
        w_t_ready = sem("w_t_ready")
        xg_ready = [sem(f"xg_ready_{k}") for k in range(RING)]
        xg_turned = sem("xg_turned")
        xg_t_ready = sem("xg_t_ready")
        h_ready = sem("h_ready")
        silu_ready = sem("silu_ready")
        y_ready = sem("y_ready")
        y_turned = sem("y_turned")
        y_t_ready = sem("y_t_ready")
        u_ready = sem("u_ready")
        rows_ready = sem("rows_ready")
        rows_stored = [sem(f"rows_stored_{k}") for k in range(RING)]
        og_ready = [sem(f"og_ready_{g}") for g in range(GROUPS)]
        s_done = sem("s_done")
        fin_ready = sem("fin_ready")
        out_stored = [sem(f"out_stored_{c}") for c in range(CHUNKS)]
        dve_step = sem("dve_step")

        block = ctx.enter_context(nc.Block())

        @block.sync
        def _(sp):
            def load_x(c):
                if c >= 2:
                    sp.wait_ge(z_ready, GROUPS * (c - 1))
                sp.dma_start(x_in[:, c % 2, :, :].rearrange("p (g j) d -> p g (j d)", j=TPG),
                             chunk_view(x_rows, c)).then_inc(x_loaded[c % 2], 16)

            def store_x1(c):
                for g in range(GROUPS):
                    sp.wait_ge(x1_ready, GROUPS * c + g + 1)
                    sp.dma_start(group_view(x1_dram[c], 0, g),
                                 x1[c % 3][:, g * TPG:(g + 1) * TPG, :].rearrange("p j d -> p (j d)")
                                 ).then_inc(x1_stored[c], 16)

            def store_block(c, b, k):
                sp.wait_ge(rows_ready, MAX_BLOCKS * c + b + 1)
                sp.dma_start(slot_dram[c][bass.ds(b * P, P), :], rows_out[:, k, :]).then_inc(rows_stored[k], 16)

            def store_out(c):
                for g in range(GROUPS):
                    sp.wait_ge(fin_ready, GROUPS * c + g + 1)
                    sp.dma_start(group_view(out_rows, c, g),
                                 fin[:, g * TPG:(g + 1) * TPG, :].rearrange("p j d -> p (j d)")
                                 ).then_inc(out_stored[c], 16)

            def store_blocks(c):
                with sp.Fori(0, MAX_BLOCKS // RING) as q:
                    for k in range(RING):
                        store_block(c, q * RING + k, k)

            load_x(0)
            with nc.allow_non_contiguous_dma(reason="the router's 1024 weights, once"):
                sp.dma_start(router_t[:], router_w.rearrange("e d -> d e")).then_inc(w_ready, 16)
            sp.dma_start(w_in_raw[:], w_in).then_inc(w_ready, 16)
            sp.dma_start(w_norm_sb[:], w_norm.rearrange("(d o) -> d o", o=1)).then_inc(w_ready, 16)
            sp.dma_start(lam_log[:], lambda_log.rearrange("(d o) -> d o", o=1)).then_inc(w_ready, 16)
            sp.dma_start(w_out_raw[:], w_out).then_inc(w_ready, 16)
            load_x(1)
            sp.dma_start(w1_raw[:], w1.rearrange("e (k p) d -> p (e k) d", p=P)).then_inc(experts_in, 16)
            sp.dma_start(w2_raw[:].rearrange("p (e k) i -> p e (k i)", k=2), w2.rearrange("e p i -> p e i")).then_inc(experts_in, 16)
            store_x1(0)
            for c in range(CHUNKS):
                if c + 2 < CHUNKS:
                    load_x(c + 2)
                if c + 1 < CHUNKS:
                    store_x1(c + 1)
                store_blocks(c)
                if c >= 1:
                    store_out(c - 1)
            store_out(CHUNKS - 1)
            for c in range(CHUNKS):
                sp.wait_ge(out_stored[c], 16 * GROUPS)

        @block.gpsimd
        def _(gp):
            nc.gpsimd.memset(ident[:], 0.0).then_inc(consts_step, 1)
            nc.gpsimd.memset(before[:], 1.0).then_inc(consts_step, 1)
            gp.wait_ge(consts_step, 2)
            nc.gpsimd.affine_select(out=ident[:], in_=ident[:], compare_op=ALU.not_equal, fill=1.0, base=0,
                                    pattern=[[-1, P]], channel_multiplier=1).then_inc(consts_ready, 1)
            nc.gpsimd.affine_select(out=before[:], in_=before[:], compare_op=ALU.is_gt, fill=0.0, base=0,
                                    pattern=[[1, P]], channel_multiplier=-1).then_inc(consts_ready, 1)
            nc.gpsimd.memset(ones[:], 1.0).then_inc(consts_ready, 1)
            nc.gpsimd.memset(one_row[:], 1.0).then_inc(consts_ready, 1)
            nc.gpsimd.memset(picked[:], 0.0).then_inc(consts_ready, 1)
            small = dict(allow_small_or_imprecise_dtypes=True)
            nc.gpsimd.iota(lane_iota[:], pattern=[[1, P]], base=0, channel_multiplier=0, **small).then_inc(consts_ready, 1)
            nc.gpsimd.iota(block_iota[:], pattern=[[0, 3], [1, MAX_BLOCKS]], base=0, channel_multiplier=0,
                           **small).then_inc(consts_ready, 1)
            nc.gpsimd.iota(token_parts[:, :, 0, :], pattern=[[0, TILES], [0, MAX_BLOCKS]], base=0,
                           channel_multiplier=1, **small).then_inc(consts_ready, 1)
            for i in range(TILES):
                for part, value in ((1, i % TPG), (2, i // TPG)):
                    nc.gpsimd.memset(token_parts[:, i, part, :], float(value)).then_inc(consts_ready, 1)
            nc.gpsimd.iota(first_key[:], pattern=[[0, TILES], [-1, E]], base=E, channel_multiplier=0,
                           **small).then_inc(consts_ready, 1)
            nc.gpsimd.iota(block_no[:], pattern=[[1, MAX_BLOCKS], [0, E]], base=0, channel_multiplier=0,
                           **small).then_inc(consts_ready, 1)

            def gather_blocks(c):
                gp.wait_ge(x1_stored[c], 16 * GROUPS)
                gp.wait_ge(tokens_known, c + 1)
                for b in range(MAX_BLOCKS):
                    n = MAX_BLOCKS * c + b
                    if n >= RING:
                        gp.wait_ge(xg_turned, n - RING + 1)
                    gp.indirect_dma_start(xg[b % RING][:], None, x1_dram[c],
                                          bass.IndirectOffsetOnAxis(ap=token_of[c % 2][:, b:b + 1], axis=0)
                                          ).then_inc(xg_ready[b % RING], 16)

            def gather_combine(c):
                for k in range(RING):
                    gp.wait_ge(rows_stored[k], 16 * (MAX_BLOCKS // RING) * (c + 1))
                for i in range(TILES):
                    if c >= 1 and i % TPG == 0:
                        gp.wait_ge(s_done, GROUPS * (c - 1) + i // TPG + 1)
                    for k in range(2):
                        gp.indirect_dma_start(og[:, k, i, :], None, slot_dram[c],
                                              bass.IndirectOffsetOnAxis(ap=slot_i[c % 3][:, k, i:i + 1], axis=0)
                                              ).then_inc(og_ready[i // TPG], 16)

            for c in range(CHUNKS):
                gather_blocks(c)
                gather_combine(c)

        CONSTS = 10 + 2 * TILES

        @block.tensor
        def _(pe):
            pe.wait_ge(consts_ready, CONSTS)
            pe.wait_ge(w_ready, 16 * 5)

            def turn_x(c, g):
                n = GROUPS * c + g
                pe.wait_ge(xn_ready, n + 1)
                if n >= 1:
                    pe.wait_ge(xn_t_ready, n)
                if g == 0 and c >= 1:
                    pe.wait_ge(x1_t_ready, GROUPS * c)
                    pe.wait_ge(w_t_ready, 12)
                t = ps_t[:].rearrange("p (q j) -> p j q", j=TPG)
                for j in range(TPG):
                    last = nc.tensor.transpose(t[:, j, :], x_norm[:, n % 2, j * D:(j + 1) * D], ident[:])
                last.then_inc(xn_turned, 1)

            def project(c, g):
                n = GROUPS * c + g
                pe.wait_ge(xn_t_ready, n + 1)
                if n >= 1:
                    pe.wait_ge(gates_ready, 3 * n)
                for k, ps in enumerate((ps_a, ps_r, ps_v)):
                    nc.tensor.matmul(ps[:], w_in_sb[:, k * D:(k + 1) * D], x_norm_t[:, n % 2, :],
                                     start=True, stop=True).then_inc(proj_ready, 1)

            def mix(c, g):
                n = GROUPS * c + g
                pe.wait_ge(state_ready, n + 1)
                if n >= 1:
                    pe.wait_ge(z_ready, n)
                st = state[:, n % 2, :].rearrange("p (q j) -> p j q", j=TPG)
                for j in range(TPG):
                    last = nc.tensor.matmul(ps_o[:, j * D:(j + 1) * D], st[:, j, :], w_out_sb[:],
                                            start=True, stop=True)
                last.then_inc(mixed, 1)

            def router(c):
                for g in range(GROUPS):
                    n = GROUPS * c + g
                    pe.wait_ge(x1_ready, n + 1)
                    if g == 0:
                        pe.wait_ge(xn_t_ready, GROUPS * (c + 1))
                    else:
                        pe.wait_ge(x1_t_ready, n)
                    for j in range(TPG):
                        last = nc.tensor.transpose(ps_t[:, j * P:(j + 1) * P], x1[c % 3][:, g * TPG + j, :], ident[:])
                    last.then_inc(x1_turned, 1)
                    pe.wait_ge(x1_t_ready, n + 1)
                    if g == 0 and c >= 1:
                        pe.wait_ge(tokens_known, c)
                    for j in range(TPG):
                        last = nc.tensor.matmul(ps_logits[:, g * TPG + j, :], x1_t[:, n % 2, j * P:(j + 1) * P],
                                                router_t[:], start=True, stop=True)
                    last.then_inc(logits_done, 1)

            def rank(c):
                pe.wait_ge(picked_ready, c + 1)
                nc.tensor.matmul(ps_rank[:], before[:], picked[:], start=True, stop=False)
                for i in range(TILES):
                    rest = TILES - i
                    last = nc.tensor.matmul(ps_rank[:, i + 1:, :], ones[:],
                                            picked[:, i:i + 1, :].to_broadcast([P, rest, E]),
                                            start=False, stop=(i == TILES - 1))
                last.then_inc(rank_ready, 1)

            def slot_tokens(c):
                for m in range(2 * TILES):
                    pe.wait_ge(hot_ready, 2 * TILES * c + m + 1)
                    last = nc.tensor.matmul(ps_token[:], lane_hot[:, m % 2, :], block_hot[:, m % 2, :, :],
                                            start=(m == 0), stop=(m == 2 * TILES - 1))
                    last.then_inc(hot_used, 1)

            def mixer(c):
                turn_x(c, 0)
                project(c, 0)
                turn_x(c, 1)
                for g in range(GROUPS):
                    if g + 1 < GROUPS:
                        project(c, g + 1)
                    if g + 2 < GROUPS:
                        turn_x(c, g + 2)
                    mix(c, g)
                router(c)
                rank(c)
                slot_tokens(c)

            def turn_weights():
                pe.wait_ge(experts_in, 32)
                pe.wait_ge(x1_t_ready, GROUPS)
                for q in range(12):
                    if q >= 1:
                        pe.wait_ge(w_t_ready, q)
                    for j in range(4):
                        m = 4 * q + j
                        raw = w1_raw[:, m, :] if m < 4 * E else w2_raw[:, m - 4 * E, :]
                        last = nc.tensor.transpose(ps_t[:, j * P:(j + 1) * P], raw, ident[:])
                    last.then_inc(w_turned, 1)

            def turn_rows(c, b, k):
                pe.wait_ge(xg_ready[k], (b - k + (MAX_BLOCKS * c + RING)) * (16 // RING))
                n = b + MAX_BLOCKS * c
                if not (isinstance(b, int) and n == 0):
                    pe.wait_ge(xg_t_ready, n)
                nc.tensor.transpose(ps_x[:, 0:P], xg[k][:], ident[:]).then_inc(xg_turned, 1)

            def up(c, b, k):
                n = b + MAX_BLOCKS * c
                pe.wait_ge(xg_t_ready, n + 1)
                if not (isinstance(n, int) and n < 2):
                    pe.wait_ge(y_ready, n - 1)
                at = pe.value_load(w1_at[c % 2][0:1, bass.ds(b, 1)], min_val=0, max_val=(E - 1) * 2 * INTER)
                nc.tensor.matmul(ps_h[k % 2][:], xg_t[:, k % 2, :], w1_t[:, bass.ds(at, 2 * INTER)],
                                 start=True, stop=True).then_inc(h_ready, 1)

            def turn_y(c, b, k):
                n = b + MAX_BLOCKS * c
                pe.wait_ge(y_ready, n + 1)
                if not (isinstance(n, int) and n < 1):
                    pe.wait_ge(y_t_ready, n)
                for j in range(2):
                    last = nc.tensor.transpose(ps_y[:, j * P:(j + 1) * P], y[:, k % 2, j * P:(j + 1) * P], ident[:])
                last.then_inc(y_turned, 1)

            def down(c, b, k):
                n = b + MAX_BLOCKS * c
                pe.wait_ge(y_t_ready, n + 1)
                if not (isinstance(n, int) and n < 1):
                    pe.wait_ge(rows_ready, n)
                at = pe.value_load(w2_at[c % 2][0:1, bass.ds(b, 1)], min_val=0, max_val=(E - 1) * D)
                for j in range(2):
                    last = nc.tensor.matmul(ps_u[:, 0:D], y_t[:, k % 2, j * P:(j + 1) * P],
                                            w2_t[:, j, bass.ds(at, D)], start=(j == 0), stop=(j == 1))
                last.then_inc(u_ready, 1)

            def step(c, t, k, lo=0, hi=MAX_BLOCKS):
                for lag, work in enumerate((turn_rows, up, turn_y, down)):
                    if isinstance(t, int) and not 0 <= t - lag < MAX_BLOCKS:
                        continue
                    work(c, t - lag, (k - lag) % RING)

            def experts(c):
                pe.wait_ge(experts_known, c + 1)
                for t in range(RING):
                    step(c, t, t)
                with pe.Fori(1, MAX_BLOCKS // RING) as q:
                    for k in range(RING):
                        step(c, q * RING + k, k)
                for t in range(MAX_BLOCKS, MAX_BLOCKS + 3):
                    step(c, t, t % RING)

            mixer(0)
            turn_weights()
            for c in range(CHUNKS):
                if c + 1 < CHUNKS:
                    mixer(c + 1)
                if c == 0:
                    pe.wait_ge(w_t_ready, 12)
                experts(c)

        @block.scalar
        def _(act):
            act.wait_ge(w_ready, 16 * 5)
            nc.scalar.activation(lam[:], lam_log[:], ACT.Sigmoid).then_inc(lam_ready, 1)

            def squares(c):
                act.wait_ge(x_loaded[c % 2], 16 * (c // 2 + 1))
                if c >= 1:
                    act.wait_ge(xn_ready, GROUPS * (c - 1) + 1)
                for i in range(TILES):
                    last = nc.scalar.activation(square_junk[:, i, :], x_in[:, c % 2, i, :], ACT.Square,
                                                accum_out=sumsq[:, i:i + 1])
                last.then_inc(sumsq_ready, 1)

            def copy_xn(c, g):
                n = GROUPS * c + g
                act.wait_ge(xn_turned, n + 1)
                if n >= 2:
                    act.wait_ge(proj_ready, 3 * (n - 1))
                nc.scalar.copy(x_norm_t[:, n % 2, :], ps_t[:]).then_inc(xn_t_ready, 1)

            def gates(c, g):
                n = GROUPS * c + g
                if n >= 2:
                    act.wait_ge(state_ready, n - 1)
                act.wait_ge(proj_ready, 3 * n + 1)
                nc.scalar.activation(tanh_a[:, n % 2, :], ps_a[:], ACT.Tanh, scale=0.5).then_inc(gates_ready, 1)
                act.wait_ge(proj_ready, 3 * n + 2)
                nc.scalar.activation(tanh_r[:, n % 2, :], ps_r[:], ACT.Tanh, scale=0.5).then_inc(gates_ready, 1)
                act.wait_ge(proj_ready, 3 * n + 3)
                nc.scalar.activation(gelu_v[:, n % 2, :], ps_v[:], ACT.Gelu).then_inc(gates_ready, 1)

            def mixer(c):
                squares(c)
                copy_xn(c, 0)
                copy_xn(c, 1)
                for g in range(GROUPS):
                    gates(c, g)
                    if g + 2 < GROUPS:
                        copy_xn(c, g + 2)
                for g in range(GROUPS):
                    n = GROUPS * c + g
                    act.wait_ge(x1_turned, n + 1)
                    if n >= 2:
                        act.wait_ge(logits_done, n - 1)
                    nc.scalar.copy(x1_t[:, n % 2, :], ps_t[:]).then_inc(x1_t_ready, 1)

            def exps(c):
                act.wait_ge(shifted_ready, c + 1)
                nc.scalar.activation(exp_logits[c % 3][:], shifted[c % 2][:], ACT.Exp)
                nc.scalar.activation(exp_gap[c % 3][:], top_gap[c % 2][:], ACT.Exp).then_inc(exps_ready, 1)

            def copy_weights():
                w1_v = w1_t[:].rearrange("p (q n) -> p q n", n=512)
                w2_v = w2_t[:].rearrange("p k (e h) -> p e k h", h=D)
                for q in range(12):
                    act.wait_ge(w_turned, q + 1)
                    if q < 8:
                        dst, src = w1_v[:, q, :], ps_t[:]
                    else:
                        m = 2 * (q - 8)
                        dst = w2_v[:, m:m + 2, :, :]
                        src = ps_t[:].rearrange("p (e k h) -> p e k h", e=2, k=2)
                    nc.scalar.copy(dst, src).then_inc(w_t_ready, 1)

            def copy_rows(c, b, k):
                n = b + MAX_BLOCKS * c
                act.wait_ge(xg_turned, n + 1)
                if not (isinstance(n, int) and n < 2):
                    act.wait_ge(h_ready, n - 1)
                nc.scalar.copy(xg_t[:, k % 2, :], ps_x[:, 0:P]).then_inc(xg_t_ready, 1)

            def gate(c, b, k):
                n = b + MAX_BLOCKS * c
                act.wait_ge(h_ready, n + 1)
                if not (isinstance(n, int) and n < 2):
                    act.wait_ge(y_ready, n - 1)
                nc.scalar.activation(silu[:, k % 2, :], ps_h[k % 2][:, 0:INTER], ACT.Silu).then_inc(silu_ready, 1)

            def copy_out(c, b, k):
                n = b + MAX_BLOCKS * c
                act.wait_ge(u_ready, n + 1)
                if not (isinstance(n, int) and n < RING):
                    act.wait_ge(rows_stored[k], (b - k + MAX_BLOCKS * c) * (16 // RING))
                nc.scalar.copy(rows_out[:, k, :], ps_u[:, 0:D]).then_inc(rows_ready, 1)

            def step(c, t, k):
                for lag, work in ((0, copy_rows), (1, gate), (3, copy_out)):
                    if isinstance(t, int) and not 0 <= t - lag < MAX_BLOCKS:
                        continue
                    work(c, t - lag, (k - lag) % RING)

            def experts(c):
                for t in range(RING):
                    step(c, t, t)
                with act.Fori(1, MAX_BLOCKS // RING) as q:
                    for k in range(RING):
                        step(c, q * RING + k, k)
                for t in range(MAX_BLOCKS, MAX_BLOCKS + 3):
                    step(c, t, t % RING)

            mixer(0)
            exps(0)
            copy_weights()
            for c in range(CHUNKS):
                if c + 1 < CHUNKS:
                    mixer(c + 1)
                    exps(c + 1)
                experts(c)

        @block.vector
        def _(dve):
            steps = [0]

            def mark(ins):
                ins.then_inc(dve_step, 1)
                steps[0] += 1

            def after_marks():
                dve.wait_ge(dve_step, steps[0])

            def link(ins):
                mark(ins)
                after_marks()

            def inverse_root(dst, src, eps, scale):
                link(nc.vector.tensor_scalar(nr_half[:], src, scale, eps, ALU.mult, ALU.add))
                link(nc.vector.tensor_scalar(nr_int[:], nr_half[:].bitcast(I32), 1, None, ALU.arith_shift_right))
                link(nc.vector.tensor_scalar(dst.bitcast(I32), nr_int[:], -1.0, RSQRT_MAGIC, ALU.mult, ALU.add))
                link(nc.vector.tensor_scalar(nr_half[:], nr_half[:], -0.5, None, ALU.mult))
                for _ in range(3):
                    link(nc.vector.tensor_tensor(nr_tmp[:], dst, dst, ALU.mult))
                    link(nc.vector.tensor_tensor(nr_tmp[:], nr_tmp[:], nr_half[:], ALU.mult))
                    link(nc.vector.scalar_tensor_tensor(dst, nr_tmp[:], 1.5, dst, ALU.add, ALU.mult))

            def layer_stats():
                mark(nc.vector.tensor_tensor(mean[:], stats[:, :, 1], stats[:, :, 4], ALU.add))
                mark(nc.vector.tensor_tensor(mean_diff[:], stats[:, :, 1], stats[:, :, 4], ALU.subtract))
                mark(nc.vector.tensor_tensor(var[:], stats[:, :, 2], stats[:, :, 5], ALU.add))
                after_marks()
                link(nc.vector.tensor_tensor(mean_diff[:], mean_diff[:], mean_diff[:], ALU.mult))
                link(nc.vector.scalar_tensor_tensor(var[:], mean_diff[:], D / 4.0, var[:], ALU.mult, ALU.add))
                inverse_root(rstd[:], var[:], LN_EPS, 1.0 / D)
                link(nc.vector.scalar_tensor_tensor(neg_mean_rstd[:], mean[:], -0.5, rstd[:], ALU.mult, ALU.mult))

            def normalise(c, g):
                n = GROUPS * c + g
                if n >= 2:
                    dve.wait_ge(xn_turned, n - 1)
                tiles = slice(g * TPG, (g + 1) * TPG)
                nc.vector.tensor_tensor(x_norm[:, n % 2, :].rearrange("p (j d) -> p j d", j=TPG),
                                        x_in[:, c % 2, tiles, :],
                                        rms_inv[:, tiles].rearrange("p (j o) -> p j o", o=1).to_broadcast([P, TPG, D]),
                                        ALU.mult).then_inc(xn_ready, 1)

            def recur(c, g):
                n = GROUPS * c + g
                if n >= 2:
                    dve.wait_ge(mixed, n - 1)
                dve.wait_ge(gates_ready, 3 * n + 1)
                mark(nc.vector.tensor_scalar(gate_a[:], tanh_a[:, n % 2, :], 0.5, 0.5, ALU.mult, ALU.add))
                dve.wait_ge(gates_ready, 3 * n + 3)
                link(nc.vector.scalar_tensor_tensor(u1[:], tanh_a[:, n % 2, :], -1.0, gelu_v[:, n % 2, :],
                                                    ALU.add, ALU.mult))
                link(nc.vector.scalar_tensor_tensor(u2[:], tanh_r[:, n % 2, :], 1.0, u1[:], ALU.add, ALU.mult))
                first = 0.0 if g % SEQ_GROUPS == 0 else state[:, (n - 1) % 2, GROUP - 1:GROUP]
                if g % SEQ_GROUPS:
                    dve.wait_ge(state_ready, n)
                nc.vector.tensor_tensor_scan(state[:, n % 2, :], gate_a[:], u2[:], first, ALU.mult, ALU.add
                                             ).then_inc(state_ready, 1)

            def residual(c, g):
                n = GROUPS * c + g
                dve.wait_ge(mixed, n + 1)
                tiles = slice(g * TPG, (g + 1) * TPG)
                nc.vector.scalar_tensor_tensor(z[:, tiles, :].rearrange("p j d -> p (j d)"),
                                               x_in[:, c % 2, tiles, :].rearrange("p j d -> p (j d)"), 2.0,
                                               ps_o[:], ALU.mult, ALU.add).then_inc(z_ready, 1)
                dve.wait_ge(z_ready, n + 1)
                for i in range(g * TPG, (g + 1) * TPG):
                    mark(nc.vector.bn_stats(stats[:, i, :], z[:, i, :]))

            def mixer(c):
                dve.wait_ge(sumsq_ready, c + 1)
                inverse_root(rms_inv[:], sumsq[:], RMS_EPS, 1.0 / D)
                normalise(c, 0)
                normalise(c, 1)
                for g in range(GROUPS):
                    recur(c, g)
                    if g + 2 < GROUPS:
                        normalise(c, g + 2)
                    residual(c, g)
                after_marks()
                layer_stats()
                if c >= 3:
                    dve.wait_ge(x1_stored[c - 3], 16 * GROUPS)
                for g in range(GROUPS):
                    for i in range(g * TPG, (g + 1) * TPG):
                        last = nc.vector.tensor_scalar(x1[c % 3][:, i, :], z[:, i, :], rstd[:, i:i + 1],
                                                       neg_mean_rstd[:, i:i + 1], ALU.mult, ALU.add)
                    last.then_inc(x1_ready, 1)

            def over_experts(v):
                return v.rearrange("p (i o) -> p i o", o=1).to_broadcast([P, TILES, E])

            def pick_top(k, values, top):
                link(nc.vector.tensor_reduce(top, values, AX.X, ALU.max))
                link(nc.vector.tensor_tensor(route_a[:], values, over_experts(top), ALU.is_equal))
                link(nc.vector.tensor_tensor(route_a[:], route_a[:], first_key[:], ALU.mult))
                link(nc.vector.tensor_reduce(route_b[:], route_a[:], AX.X, ALU.max))
                link(nc.vector.tensor_tensor(pick[:, k], first_key[:], over_experts(route_b[:]), ALU.is_equal))

            def route(c):
                dve.wait_ge(logits_done, GROUPS * (c + 1))
                link(nc.vector.tensor_copy(logits[:], ps_logits[:]))
                pick_top(0, logits[:], top1[:])
                mark(nc.vector.tensor_tensor(shifted[c % 2][:], logits[:], over_experts(top1[:]), ALU.subtract))
                after_marks()
                link(nc.vector.scalar_tensor_tensor(logits[:], pick[:, 0], LOWEST, logits[:], ALU.mult, ALU.add))
                pick_top(1, logits[:], top2[:])
                nc.vector.tensor_tensor(picked[:, 0:TILES, :], pick[:, 0], pick[:, 1], ALU.add
                                        ).then_inc(picked_ready, 1)
                nc.vector.tensor_tensor(top_gap[c % 2][:], top2[:], top1[:], ALU.subtract).then_inc(shifted_ready, 1)
                dve.wait_ge(rank_ready, c + 1)
                link(nc.vector.tensor_scalar(count_i[:], ps_rank[:, TILES, :], float(P - 1), None, ALU.add))
                link(nc.vector.tensor_scalar(count_i[:], count_i[:], 7, None, ALU.arith_shift_right))
                link(nc.vector.tensor_copy(blocks_of[:], count_i[:]))
                link(nc.vector.tensor_tensor_scan(block_end[:], one_row[:], blocks_of[:], 0.0, ALU.mult, ALU.add))
                link(nc.vector.tensor_tensor(slot_base[:], block_end[:], blocks_of[:], ALU.subtract))
                link(nc.vector.tensor_scalar(slot_base[:], slot_base[:], float(P), None, ALU.mult))
                link(nc.vector.tensor_tensor(route_a[:], ps_rank[:, 0:TILES, :],
                                             slot_base[:].rearrange("p (o e) -> p o e", o=1).to_broadcast([P, TILES, E]),
                                             ALU.add))
                for k in range(2):
                    link(nc.vector.tensor_tensor(pick[:, k], pick[:, k], route_a[:], ALU.mult))
                    link(nc.vector.tensor_reduce(slot_f[:, k], pick[:, k], AX.X, ALU.add))
                slots = slot_i[c % 3]
                link(nc.vector.tensor_copy(slots[:], slot_f[:]))
                flat = slots[:].rearrange("p k i -> p (k i)")
                mark(nc.vector.tensor_scalar(part_i[:, 0], flat, 7, None, ALU.arith_shift_right))
                mark(nc.vector.tensor_scalar(part_i[:, 1], flat, P - 1, None, ALU.bitwise_and))
                after_marks()
                mark(nc.vector.tensor_copy(slot_block[:], part_i[:, 0]))
                mark(nc.vector.tensor_copy(slot_lane[:], part_i[:, 1]))
                after_marks()
                link(nc.vector.tensor_tensor(ended[:], block_no[:],
                                             block_end[:].rearrange("p (o e) -> p o e", o=1)
                                             .to_broadcast([P, MAX_BLOCKS, E]), ALU.is_ge))
                link(nc.vector.tensor_reduce(expert_f[:], ended[:], AX.X, ALU.add))
                link(nc.vector.tensor_scalar(expert_f[:], expert_f[:], float(E - 1), None, ALU.min))
                nc.vector.tensor_scalar(w1_at[c % 2][:], expert_f[:], float(2 * INTER), None, ALU.mult)
                nc.vector.tensor_scalar(w2_at[c % 2][:], expert_f[:], float(D), None, ALU.mult
                                        ).then_inc(experts_known, 1)
                for m in range(2 * TILES):
                    n = 2 * TILES * c + m
                    if n >= 2:
                        dve.wait_ge(hot_used, n - 1)
                    nc.vector.tensor_scalar(lane_hot[:, m % 2, :], lane_iota[:], slot_lane[:, m:m + 1], None,
                                            ALU.is_equal)
                    nc.vector.scalar_tensor_tensor(block_hot[:, m % 2].rearrange("p a b -> p (a b)"),
                                                   block_iota[:].rearrange("p a b -> p (a b)"),
                                                   slot_block[:, m:m + 1],
                                                   token_parts[:, m % TILES].rearrange("p a b -> p (a b)"),
                                                   ALU.is_equal, ALU.mult).then_inc(hot_ready, 1)
                dve.wait_ge(hot_used, 2 * TILES * (c + 1))
                link(nc.vector.tensor_copy(token_ps[:], ps_token[:]))
                link(nc.vector.scalar_tensor_tensor(token_pj[:], token_ps[:, 0], float(TPG), token_ps[:, 1],
                                                    ALU.mult, ALU.add))
                if c >= 2:
                    for k in range(RING):
                        dve.wait_ge(xg_ready[k], 16 * (MAX_BLOCKS // RING) * (c - 1))
                nc.vector.scalar_tensor_tensor(token_of[c % 2][:], token_ps[:, 2], float(GROUP), token_pj[:],
                                               ALU.mult, ALU.add).then_inc(tokens_known, 1)

            def product(c, b, k):
                n = b + MAX_BLOCKS * c
                dve.wait_ge(silu_ready, n + 1)
                if not (isinstance(n, int) and n < 2):
                    dve.wait_ge(y_turned, n - 1)
                nc.vector.tensor_tensor(y[:, k % 2, :], silu[:, k % 2, :], ps_h[k % 2][:, INTER:2 * INTER],
                                        ALU.mult).then_inc(y_ready, 1)

            def copy_y(c, b, k):
                n = b + MAX_BLOCKS * c
                dve.wait_ge(y_turned, n + 1)
                if not (isinstance(n, int) and n < 2):
                    dve.wait_ge(u_ready, n - 1)
                nc.vector.tensor_copy(y_t[:, k % 2, :], ps_y[:, 0:INTER]).then_inc(y_t_ready, 1)

            def step(c, t, k):
                for lag, work in ((2, copy_y), (1, product)):
                    if isinstance(t, int) and not 0 <= t - lag < MAX_BLOCKS:
                        continue
                    work(c, t - lag, (k - lag) % RING)

            def experts(c):
                for t in range(RING):
                    step(c, t, t)
                with dve.Fori(1, MAX_BLOCKS // RING) as q:
                    for k in range(RING):
                        step(c, q * RING + k, k)
                for t in range(MAX_BLOCKS, MAX_BLOCKS + 3):
                    step(c, t, t % RING)

            def combine(c):
                dve.wait_ge(exps_ready, c + 1)
                link(nc.vector.tensor_reduce(route_b[:], exp_logits[c % 3][:], AX.X, ALU.add))
                link(nc.vector.reciprocal(weight[:, 0], route_b[:]))
                link(nc.vector.tensor_tensor(weight[:, 1], weight[:, 0], exp_gap[c % 3][:], ALU.mult))
                for g in range(GROUPS):
                    dve.wait_ge(og_ready[g], 16 * 2 * TPG * (c + 1))
                    for i in range(g * TPG, (g + 1) * TPG):
                        mark(nc.vector.scalar_tensor_tensor(s[:, i, :], og[:, 0, i, :], weight[:, 0, i:i + 1],
                                                            x1[c % 3][:, i, :], ALU.mult, ALU.add))
                    after_marks()
                    for i in range(g * TPG, (g + 1) * TPG):
                        last = nc.vector.scalar_tensor_tensor(s[:, i, :], og[:, 1, i, :], weight[:, 1, i:i + 1],
                                                              s[:, i, :], ALU.mult, ALU.add)
                    last.then_inc(s_done, 1)
                    dve.wait_ge(s_done, GROUPS * c + g + 1)
                    for i in range(g * TPG, (g + 1) * TPG):
                        mark(nc.vector.bn_stats(stats[:, i, :], s[:, i, :]))
                after_marks()
                layer_stats()
                if c >= 1:
                    dve.wait_ge(out_stored[c - 1], 16 * GROUPS)
                for g in range(GROUPS):
                    for i in range(g * TPG, (g + 1) * TPG):
                        last = nc.vector.tensor_scalar(fin[:, i, :], s[:, i, :], rstd[:, i:i + 1],
                                                       neg_mean_rstd[:, i:i + 1], ALU.mult, ALU.add)
                    last.then_inc(fin_ready, 1)

            dve.wait_ge(w_ready, 16 * 5)
            dve.wait_ge(consts_ready, CONSTS)
            dve.wait_ge(lam_ready, 1)
            mark(nc.vector.tensor_scalar(w_in_sb[:], w_in_raw[:], w_norm_sb[:], None, ALU.mult))
            mark(nc.vector.tensor_scalar(w_out_sb[:], w_out_raw[:], lam[:], -0.25, ALU.mult, ALU.mult))
            after_marks()
            mixer(0)
            route(0)
            for c in range(CHUNKS):
                if c + 1 < CHUNKS:
                    mixer(c + 1)
                    route(c + 1)
                experts(c)
                if c >= 1:
                    combine(c - 1)
            combine(CHUNKS - 1)


_INS = ["L0_attn_x", "L0_attn_w_norm", "L0_attn_W_in", "L0_attn_lambda_log", "L0_attn_W_out",
        "L0_ffn_w1", "L0_ffn_w2", "L0_ffn_router_w"]


def kernel(**inputs):
    import numpy as _np
    import concourse.bacc as _bacc
    from concourse import mybir as _mybir
    from concourse.bass_utils import run_bass_kernel_spmd as _run

    nc = _bacc.Bacc("TRN2", target_bir_lowering=False, num_devices=1)
    arrays, args = {}, []
    for name in _INS:
        a = _np.ascontiguousarray(inputs[name])
        arrays[f"in_{name}"] = a
        args.append(nc.dram_tensor(f"in_{name}", a.shape, _mybir.dt.from_np(a.dtype), kind="ExternalInput").ap())
    out = nc.dram_tensor("out", (8, 1024, 128), _mybir.dt.from_np(_np.dtype("float32")), kind="ExternalOutput").ap()
    moe_layer(nc, *args, out)
    r = _run(nc, [arrays], core_ids=[0])
    return r.results[0]["out"]
```

```python
import concourse.bass as bass
from concourse import mybir
from contextlib import ExitStack

F32 = mybir.dt.float32
BF16 = mybir.dt.bfloat16
I32 = mybir.dt.int32
ALU = mybir.AluOpType
ACT = mybir.ActivationFunctionType
AX = mybir.AxisListType

P = 128
D = 128
E = 8
INTER = 256
TOKENS = 8 * 1024
CHUNK = 2048
CHUNKS = TOKENS // CHUNK
TILES = CHUNK // P
GROUP = 512
GROUPS = CHUNK // GROUP
TPG = GROUP // P
SEQ_GROUPS = 1024 // GROUP
MAX_BLOCKS = 2 * TILES + E - 1
ROWS_RING = 4
GATHER_RING = 8
W_STRIDE = 2 * INTER + 2 * D
HOTS = 4
HOT_RING = 8

RMS_EPS = 1e-6
LN_EPS = 1e-5
LOWEST = -3.0e38
RSQRT_MAGIC = float(0x5F3759DF)

MIXER_PARTS = {t: [] for t in range(64)}


def _at(tick, *part):
    MIXER_PARTS[tick].append(part)


_at(0, "squares", 0)
_at(1, "rms", 0)
for _g in range(GROUPS):
    _at(1 + 3 * _g, "normalise", _g)
    _at(2 + 3 * _g, "turn_x", _g)
    for _k in range(3):
        _at(3 + 3 * _g + _k, "project", (_g, _k))
for _g in range(GROUPS):
    _s = 10 + 6 * (_g // 2) + 2 * (_g % 2)
    if _g % 2 == 0:
        _at(_s - 1, "gelu", _g)
    _at(_s, "recur", _g)
    _at(_s + 1, "scan", _g)
    _at(_s + 2, "mix", _g)
    _at(_s + 3, "residual", _g)
_at(22, "x1_stats", 0)
for _g in range(GROUPS):
    _at(22 + _g, "x1", _g)
    _at(23 + _g, "turn_x1", _g)
    _at(24 + _g, "logits", _g)
_at(28, "pick", 0)
_at(29, "pick", 1)
_at(30, "rank", 0)
_at(31, "slots", 0)
_at(32, "block_experts", 0)
for _m in range(2 * TILES // HOTS):
    _at(33 + _m, "hots", _m)
LAST_MIXER = 33 + 2 * TILES // HOTS
_at(LAST_MIXER, "token_lists", 0)

COMBINE_PARTS = {t: [] for t in range(64)}
COMBINE_PARTS[10].append(("weights", 0))
for _g in range(GROUPS):
    COMBINE_PARTS[11 + 8 * _g].append(("first", _g))
    COMBINE_PARTS[12 + 8 * _g].append(("second", _g))
COMBINE_PARTS[37].append(("out_stats", 0))
for _g in range(GROUPS):
    COMBINE_PARTS[38 + _g].append(("out", _g))
TICKS = max(MAX_BLOCKS + 3, LAST_MIXER + 1, 42)


def _tick_of(*part):
    return next(t for t, parts in MIXER_PARTS.items() if part in parts)


MIXED_BEFORE_TURN = [sum(_tick_of("mix", h) < _tick_of("turn_x", g) for h in range(GROUPS)) for g in range(GROUPS)]
TURNED_BEFORE_MIX = [sum(_tick_of("turn_x", h) <= _tick_of("mix", g) for h in range(GROUPS)) for g in range(GROUPS)]


def run_parts(table, tick, chunk, work):
    if 0 <= chunk < CHUNKS:
        for name, arg in table[tick]:
            if name in work:
                work[name](chunk, arg)


def moe_layer(nc, x, w_norm, w_in, lambda_log, w_out, w1, w2, router_w, out):
    x_rows = x.rearrange("b t d -> (b t) d")
    out_rows = out.rearrange("b t d -> (b t) d")

    def chunk_view(rows, c):
        return rows[c * CHUNK:(c + 1) * CHUNK, :].rearrange("(g p j) d -> p g (j d)", p=P, j=TPG)

    def group_view(rows, c, g):
        r0 = c * CHUNK + g * GROUP
        return rows[r0:r0 + GROUP, :].rearrange("(p j) d -> p (j d)", j=TPG)

    x1_dram = [nc.dram_tensor(f"x1_rows_{c}", [CHUNK, D], F32, kind="Internal").ap() for c in range(CHUNKS)]
    slot_dram = [nc.dram_tensor(f"slot_rows_{c}", [MAX_BLOCKS * P, D], F32, kind="Internal").ap()
                 for c in range(CHUNKS)]

    with ExitStack() as ctx:
        def sb(name, shape, dt=F32):
            return ctx.enter_context(nc.sbuf_tensor(name, shape, dt))

        def bank(name):
            return ctx.enter_context(nc.psum_tensor(name, [P, 512], F32))

        def sem(name):
            return ctx.enter_context(nc.semaphore(name))

        w_in_raw = sb("w_in_raw", [P, 3 * D])
        w_in_sb = sb("w_in_sb", [P, 3 * D])
        w_out_sb = sb("w_out_sb", [P, D])
        w_norm_sb = sb("w_norm_sb", [P, 1])
        lam_log = sb("lam_log", [P, 1])
        lam = sb("lam", [P, 1])
        w_out_raw = sb("w_out_raw", [P, D])
        router_t = sb("router_t", [P, E])
        w_t = sb("w_t", [P, E * W_STRIDE])
        ident = sb("ident", [P, P])
        before = sb("before", [P, P], BF16)
        ones = sb("ones", [P, P], BF16)
        lane_iota = sb("lane_iota", [P, P], BF16)
        block_iota = sb("block_iota", [P, 3, MAX_BLOCKS], BF16)
        token_parts = sb("token_parts", [P, TILES, 3, MAX_BLOCKS], BF16)
        first_key = sb("first_key", [P, TILES, E])
        block_no = sb("block_no", [P, MAX_BLOCKS, E])

        x_in = sb("x_in", [P, 2, TILES, D])
        square_junk = sb("square_junk", [P, TILES, D])
        sumsq = sb("sumsq", [P, TILES])
        rms_inv = sb("rms_inv", [P, TILES])
        nr_half = sb("nr_half", [P, TILES])
        nr_tmp = sb("nr_tmp", [P, TILES])
        nr_int = sb("nr_int", [P, TILES], I32)
        x_norm = sb("x_norm", [P, 2, GROUP])
        x_norm_t = sb("x_norm_t", [P, 2, GROUP])
        tanh_a = sb("tanh_a", [P, GROUPS, GROUP])
        tanh_r = sb("tanh_r", [P, GROUPS, GROUP])
        value = sb("value", [P, 2, GROUP])
        gelu_v = sb("gelu_v", [P, 2, GROUP])
        gate_a = sb("gate_a", [P, GROUP])
        u1 = sb("u1", [P, GROUP])
        u2 = sb("u2", [P, GROUP])
        state = sb("state", [P, 2, GROUP])
        z = sb("z", [P, TILES, D])
        stats = sb("stats", [P, TILES, 6])
        mean = sb("mean", [P, TILES])
        mean_diff = sb("mean_diff", [P, TILES])
        var = sb("var", [P, TILES])
        rstd = sb("rstd", [P, TILES])
        neg_mean_rstd = sb("neg_mean_rstd", [P, TILES])
        x1 = [sb(f"x1_{k}", [P, TILES, D]) for k in range(3)]
        x1_t = sb("x1_t", [P, 2, GROUP])

        logits = sb("logits", [P, TILES, E])
        top1 = sb("top1", [P, TILES])
        top2 = sb("top2", [P, TILES])
        top_gap = [sb(f"top_gap_{k}", [P, TILES]) for k in range(2)]
        route_a = sb("route_a", [P, TILES, E])
        route_b = sb("route_b", [P, TILES])
        pick = sb("pick", [P, 2, TILES, E])
        picked = sb("picked", [P, TILES + 1, E], BF16)
        shifted = [sb(f"shifted_{k}", [P, TILES, E]) for k in range(2)]
        exp_logits = [sb(f"exp_logits_{k}", [P, TILES, E]) for k in range(3)]
        exp_gap = [sb(f"exp_gap_{k}", [P, TILES]) for k in range(3)]
        weight = sb("weight", [P, 2, TILES])
        count_i = sb("count_i", [P, E], I32)
        blocks_of = sb("blocks_of", [P, E])
        block_end = sb("block_end", [P, E])
        slot_base = sb("slot_base", [P, E])
        one_row = sb("one_row", [P, E])
        slot_f = sb("slot_f", [P, 2, TILES])
        slot_i = [sb(f"slot_i_{k}", [P, 2, TILES], I32) for k in range(3)]
        part_i = sb("part_i", [P, 2, 2 * TILES], I32)
        slot_block = sb("slot_block", [P, 2 * TILES])
        slot_lane = sb("slot_lane", [P, 2 * TILES])
        ended = sb("ended", [P, MAX_BLOCKS, E])
        expert_f = sb("expert_f", [P, MAX_BLOCKS])
        w_at = [sb(f"w_at_{k}", [P, MAX_BLOCKS], I32) for k in range(2)]
        lane_hot = sb("lane_hot", [P, HOT_RING, P], BF16)
        block_hot = sb("block_hot", [P, HOT_RING, 3, MAX_BLOCKS], BF16)
        token_pj = sb("token_pj", [P, MAX_BLOCKS])
        token_ps = sb("token_ps", [P, 3, MAX_BLOCKS])
        token_of = [sb(f"token_of_{k}", [P, MAX_BLOCKS], I32) for k in range(2)]

        xg = [sb(f"xg_{k}", [P, D]) for k in range(GATHER_RING)]
        xg_t = sb("xg_t", [P, 2, P])
        silu = sb("silu", [P, 2, INTER])
        y = sb("y", [P, 2, INTER])
        y_t = sb("y_t", [P, 2, INTER])
        rows_out = sb("rows_out", [P, ROWS_RING, D])

        og = sb("og", [P, 2, TILES, D])
        s = sb("s", [P, TILES, D])
        out_bn = sb("out_bn", [P, TILES, 6])
        out_rstd = sb("out_rstd", [P, TILES])
        out_shift = sb("out_shift", [P, TILES])
        fin = sb("fin", [P, TILES, D])
        w1_raw = og[:].rearrange("p k i d -> p (k i) d")
        w2_raw = s

        ps_t = bank("ps_t")
        ps_p = [bank("ps_p0"), bank("ps_p1")]
        ps_h = [bank("ps_h0"), bank("ps_h1")]
        ps_x = bank("ps_x")
        ps_y = bank("ps_y")
        ps_u = bank("ps_u")
        ps_q = ps_p[0]
        ps_logits = ps_q[:, 0:TILES * E].rearrange("p (i e) -> p i e", e=E)
        ps_rank = ps_q[:, 0:(TILES + 1) * E].rearrange("p (i e) -> p i e", e=E)
        ps_token = ps_q[:, 0:3 * MAX_BLOCKS].rearrange("p (a b) -> p a b", a=3)

        w_ready = sem("w_ready")
        experts_in = sem("experts_in")
        consts_ready = sem("consts_ready")
        consts_step = sem("consts_step")
        lam_ready = sem("lam_ready")
        x_loaded = [sem(f"x_loaded_{k}") for k in range(2)]
        sumsq_ready = sem("sumsq_ready")
        xn_ready = sem("xn_ready")
        xn_turned = sem("xn_turned")
        xn_t_ready = sem("xn_t_ready")
        proj_ready = sem("proj_ready")
        gates_ready = sem("gates_ready")
        gelu_ready = sem("gelu_ready")
        state_ready = sem("state_ready")
        mixed = sem("mixed")
        z_ready = sem("z_ready")
        x1_stats = sem("x1_stats")
        x1_ready = sem("x1_ready")
        x1_stored = [sem(f"x1_stored_{c}") for c in range(CHUNKS)]
        x1_turned = sem("x1_turned")
        x1_t_ready = sem("x1_t_ready")
        logits_done = sem("logits_done")
        logits_read = sem("logits_read")
        shifted_ready = sem("shifted_ready")
        exps_ready = sem("exps_ready")
        picked_ready = sem("picked_ready")
        rank_ready = sem("rank_ready")
        experts_known = sem("experts_known")
        hot_ready = sem("hot_ready")
        hot_used = sem("hot_used")
        token_sum = sem("token_sum")
        tokens_known = sem("tokens_known")
        w_turned = sem("w_turned")
        w_t_ready = sem("w_t_ready")
        xg_ready = [sem(f"xg_ready_{k}") for k in range(GATHER_RING)]
        xg_turned = sem("xg_turned")
        xg_t_ready = sem("xg_t_ready")
        h_ready = sem("h_ready")
        silu_ready = sem("silu_ready")
        y_ready = sem("y_ready")
        y_turned = sem("y_turned")
        y_t_ready = sem("y_t_ready")
        u_ready = sem("u_ready")
        rows_ready = sem("rows_ready")
        rank_read = sem("rank_read")
        rows_stored = [sem(f"rows_stored_{k}") for k in range(ROWS_RING)]
        og_ready = [sem(f"og_ready_{g}") for g in range(GROUPS)]
        s_done = sem("s_done")
        out_stats = sem("out_stats")
        fin_ready = sem("fin_ready")
        out_stored = [sem(f"out_stored_{c}") for c in range(CHUNKS)]
        dve_step = sem("dve_step")

        def uses_before(n, ring):
            return n // ring

        def filled(c, ring, k):
            return (MAX_BLOCKS * (c + 1) - k + ring - 1) // ring

        block = ctx.enter_context(nc.Block())

        @block.sync
        def _(sp):
            def load_x(c):
                if c >= 2:
                    sp.wait_ge(z_ready, GROUPS * (c - 1))
                sp.dma_start(x_in[:, c % 2, :, :].rearrange("p (g j) d -> p g (j d)", j=TPG),
                             chunk_view(x_rows, c)).then_inc(x_loaded[c % 2], 16)

            def store_x1(c, g):
                sp.wait_ge(x1_ready, GROUPS * c + g + 1)
                sp.dma_start(group_view(x1_dram[c], 0, g),
                             x1[c % 3][:, g * TPG:(g + 1) * TPG, :].rearrange("p j d -> p (j d)")
                             ).then_inc(x1_stored[c], 16)

            def next_x(c, g):
                if g == GROUPS - 1 and c + 2 < CHUNKS:
                    load_x(c + 2)

            def store_block(c, b):
                n = MAX_BLOCKS * c + b
                sp.wait_ge(rows_ready, n + 1)
                sp.dma_start(slot_dram[c][b * P:(b + 1) * P, :], rows_out[:, n % ROWS_RING, :]
                             ).then_inc(rows_stored[n % ROWS_RING], 16)

            def store_out(c, g):
                sp.wait_ge(fin_ready, GROUPS * c + g + 1)
                sp.dma_start(group_view(out_rows, c, g),
                             fin[:, g * TPG:(g + 1) * TPG, :].rearrange("p j d -> p (j d)")
                             ).then_inc(out_stored[c], 16)

            load_x(0)
            with nc.allow_non_contiguous_dma(reason="the router's 1024 weights, once"):
                sp.dma_start(router_t[:], router_w.rearrange("e d -> d e")).then_inc(w_ready, 16)
            sp.dma_start(w_in_raw[:], w_in).then_inc(w_ready, 16)
            sp.dma_start(w_norm_sb[:], w_norm.rearrange("(d o) -> d o", o=1)).then_inc(w_ready, 16)
            sp.dma_start(lam_log[:], lambda_log.rearrange("(d o) -> d o", o=1)).then_inc(w_ready, 16)
            sp.dma_start(w_out_raw[:], w_out).then_inc(w_ready, 16)
            load_x(1)
            sp.dma_start(w1_raw, w1.rearrange("e (k p) d -> p (e k) d", p=P)).then_inc(experts_in, 16)
            sp.dma_start(w2_raw[:].rearrange("p (e k) i -> p e (k i)", k=2), w2.rearrange("e p i -> p e i")).then_inc(experts_in, 16)
            for c in range(-1, CHUNKS + 1):
                for t in range(TICKS):
                    run_parts(MIXER_PARTS, t, c + 1, {"residual": next_x, "turn_x1": store_x1})
                    if 0 <= c < CHUNKS and 0 <= t - 3 < MAX_BLOCKS:
                        store_block(c, t - 3)
                    run_parts(COMBINE_PARTS, t, c - 1, {"out": store_out})
            for c in range(CHUNKS):
                sp.wait_ge(out_stored[c], 16 * GROUPS)

        @block.gpsimd
        def _(gp):
            nc.gpsimd.memset(ident[:], 0.0).then_inc(consts_step, 1)
            nc.gpsimd.memset(before[:], 1.0).then_inc(consts_step, 1)
            gp.wait_ge(consts_step, 2)
            nc.gpsimd.affine_select(out=ident[:], in_=ident[:], compare_op=ALU.not_equal, fill=1.0, base=0,
                                    pattern=[[-1, P]], channel_multiplier=1).then_inc(consts_ready, 1)
            nc.gpsimd.affine_select(out=before[:], in_=before[:], compare_op=ALU.is_gt, fill=0.0, base=0,
                                    pattern=[[1, P]], channel_multiplier=-1).then_inc(consts_ready, 1)
            nc.gpsimd.memset(ones[:], 1.0).then_inc(consts_ready, 1)
            nc.gpsimd.memset(one_row[:], 1.0).then_inc(consts_ready, 1)
            nc.gpsimd.memset(picked[:], 0.0).then_inc(consts_ready, 1)
            small = dict(allow_small_or_imprecise_dtypes=True)
            nc.gpsimd.iota(lane_iota[:], pattern=[[1, P]], base=0, channel_multiplier=0, **small).then_inc(consts_ready, 1)
            nc.gpsimd.iota(block_iota[:], pattern=[[0, 3], [1, MAX_BLOCKS]], base=0, channel_multiplier=0,
                           **small).then_inc(consts_ready, 1)
            nc.gpsimd.iota(token_parts[:, :, 0, :], pattern=[[0, TILES], [0, MAX_BLOCKS]], base=0,
                           channel_multiplier=1, **small).then_inc(consts_ready, 1)
            for i in range(TILES):
                for part, value in ((1, i % TPG), (2, i // TPG)):
                    nc.gpsimd.memset(token_parts[:, i, part, :], float(value)).then_inc(consts_ready, 1)
            nc.gpsimd.iota(first_key[:], pattern=[[0, TILES], [-1, E]], base=E, channel_multiplier=0,
                           **small).then_inc(consts_ready, 1)
            nc.gpsimd.iota(block_no[:], pattern=[[1, MAX_BLOCKS], [0, E]], base=0, channel_multiplier=0,
                           **small).then_inc(consts_ready, 1)

            def gather_block(c, b):
                n = MAX_BLOCKS * c + b
                if b == 0:
                    gp.wait_ge(x1_stored[c], 16 * GROUPS)
                    gp.wait_ge(tokens_known, c + 1)
                if n >= GATHER_RING:
                    gp.wait_ge(xg_turned, n - GATHER_RING + 1)
                gp.indirect_dma_start(xg[n % GATHER_RING][:], None, x1_dram[c],
                                      bass.IndirectOffsetOnAxis(ap=token_of[c % 2][:, b:b + 1], axis=0)
                                      ).then_inc(xg_ready[n % GATHER_RING], 16)

            def gather_result(c, m):
                k, i = m % 2, m // 2
                if m == 0:
                    for r in range(ROWS_RING):
                        gp.wait_ge(rows_stored[r], 16 * filled(c, ROWS_RING, r))
                if c >= 1 and m % (2 * TPG) == 0:
                    gp.wait_ge(s_done, GROUPS * (c - 1) + i // TPG + 1)
                gp.indirect_dma_start(og[:, k, i, :], None, slot_dram[c],
                                      bass.IndirectOffsetOnAxis(ap=slot_i[c % 3][:, k, i:i + 1], axis=0)
                                      ).then_inc(og_ready[i // TPG], 16)

            for c in range(CHUNKS + 1):
                for b in range(MAX_BLOCKS):
                    if c < CHUNKS:
                        gather_block(c, b)
                    if c >= 1 and b < 2 * TILES:
                        gather_result(c - 1, b)

        PE = mybir.EngineType.PE
        CONSTS = 10 + 2 * TILES

        @block.tensor
        def _(pe):
            pe.wait_ge(consts_ready, CONSTS)
            pe.wait_ge(w_ready, 16 * 5)

            def turn_x(c, g):
                n = GROUPS * c + g
                pe.wait_ge(xn_ready, n + 1)
                if g == 0 and c == 1:
                    pe.wait_ge(w_t_ready, 12)
                elif g == 0 and c >= 2:
                    pe.wait_ge(x1_t_ready, n)
                elif g >= 1:
                    pe.wait_ge(xn_t_ready, n)
                if MIXED_BEFORE_TURN[g]:
                    pe.wait_ge(z_ready, GROUPS * c + MIXED_BEFORE_TURN[g])
                t = ps_t[:].rearrange("p (q j) -> p j q", j=TPG)
                for j in range(TPG):
                    last = nc.tensor.transpose(t[:, j, :], x_norm[:, n % 2, j * D:(j + 1) * D], ident[:])
                last.then_inc(xn_turned, 1)

            def project(c, g_k):
                g, k = g_k
                n = GROUPS * c + g
                m = 3 * n + k
                if k == 0:
                    pe.wait_ge(xn_t_ready, n + 1)
                if m >= 2:
                    pe.wait_ge(gates_ready, m - 1)
                if c >= 1 and g == 0 and k == 0:
                    pe.wait_ge(tokens_known, c)
                nc.tensor.matmul(ps_p[m % 2][:], w_in_sb[:, k * D:(k + 1) * D], x_norm_t[:, n % 2, :],
                                 start=True, stop=True).then_inc(proj_ready, 1)

            def mix(c, g):
                n = GROUPS * c + g
                pe.wait_ge(state_ready, n + 1)
                pe.wait_ge(xn_t_ready, GROUPS * c + TURNED_BEFORE_MIX[g])
                if n >= 1:
                    pe.wait_ge(z_ready, n)
                st = state[:, n % 2, :].rearrange("p (q j) -> p j q", j=TPG)
                for j in range(TPG):
                    last = nc.tensor.matmul(ps_t[:, j * D:(j + 1) * D], st[:, j, :], w_out_sb[:],
                                            start=True, stop=True)
                last.then_inc(mixed, 1)

            def turn_x1(c, g):
                n = GROUPS * c + g
                pe.wait_ge(x1_ready, n + 1)
                if g == 0:
                    pe.wait_ge(z_ready, GROUPS * (c + 1))
                else:
                    pe.wait_ge(x1_t_ready, n)
                for j in range(TPG):
                    last = nc.tensor.transpose(ps_t[:, j * P:(j + 1) * P], x1[c % 3][:, g * TPG + j, :], ident[:])
                last.then_inc(x1_turned, 1)

            def logits_of(c, g):
                n = GROUPS * c + g
                pe.wait_ge(x1_t_ready, n + 1)
                if g == 0:
                    pe.wait_ge(gates_ready, 3 * GROUPS * (c + 1))
                for j in range(TPG):
                    last = nc.tensor.matmul(ps_logits[:, g * TPG + j, :], x1_t[:, n % 2, j * P:(j + 1) * P],
                                            router_t[:], start=True, stop=True)
                last.then_inc(logits_done, 1)

            def rank(c, _):
                pe.wait_ge(logits_read, c + 1)
                pe.wait_ge(picked_ready, c + 1)
                nc.tensor.matmul(ps_rank[:], before[:], picked[:], start=True, stop=False)
                for i in range(TILES):
                    rest = TILES - i
                    last = nc.tensor.matmul(ps_rank[:, i + 1:, :], ones[:],
                                            picked[:, i:i + 1, :].to_broadcast([P, rest, E]),
                                            start=False, stop=(i == TILES - 1))
                last.then_inc(rank_ready, 1)

            def hots(c, q):
                if q == 0:
                    pe.wait_ge(rank_read, c + 1)
                for m in range(q * HOTS, (q + 1) * HOTS):
                    pe.wait_ge(hot_ready, 2 * TILES * c + m + 1)
                    nc.tensor.matmul(ps_token[:], lane_hot[:, m % HOT_RING, :], block_hot[:, m % HOT_RING, :, :],
                                     start=(m == 0), stop=(m == 2 * TILES - 1)).then_inc(hot_used, 1)

            def turn_weights():
                pe.wait_ge(experts_in, 32)
                pe.wait_ge(x1_t_ready, GROUPS)
                for q in range(12):
                    if q >= 1:
                        pe.wait_ge(w_t_ready, q)
                    for j in range(4):
                        m = 4 * q + j
                        raw = w1_raw[:, m, :] if m < 4 * E else w2_raw[:, m - 4 * E, :]
                        last = nc.tensor.transpose(ps_t[:, j * P:(j + 1) * P], raw, ident[:])
                    last.then_inc(w_turned, 1)

            weights_at = {}

            def up(c, b):
                n = MAX_BLOCKS * c + b
                weights_at[b] = nc.values_load(w_at[c % 2][0:1, b:b + 1], engines=(PE,), min_val=0,
                                               max_val=(E - 1) * W_STRIDE,
                                               skip_runtime_bounds_check_because="the expert is capped at E - 1")
                pe.wait_ge(xg_t_ready, n + 1)
                nc.tensor.matmul(ps_h[n % 2][:], xg_t[:, n % 2, :], w_t[:, bass.ds(weights_at[b], 2 * INTER)],
                                 start=True, stop=True).then_inc(h_ready, 1)

            def turn_rows(c, b):
                n = MAX_BLOCKS * c + b
                pe.wait_ge(xg_ready[n % GATHER_RING], 16 * (uses_before(n, GATHER_RING) + 1))
                if b == 0 and n >= 1:
                    pe.wait_ge(xg_t_ready, n)
                nc.tensor.transpose(ps_x[:, 0:P], xg[n % GATHER_RING][:], ident[:]).then_inc(xg_turned, 1)

            def down(c, b):
                n = MAX_BLOCKS * c + b
                pe.wait_ge(y_t_ready, n + 1)
                at = weights_at.pop(b)
                for j in range(2):
                    last = nc.tensor.matmul(ps_u[:, 0:D], y_t[:, n % 2, j * P:(j + 1) * P],
                                            w_t[:, bass.ds(at + (2 * INTER + j * D), D)],
                                            start=(j == 0), stop=(j == 1))
                last.then_inc(u_ready, 1)

            def turn_y(c, b):
                n = MAX_BLOCKS * c + b
                pe.wait_ge(y_ready, n + 1)
                for j in range(2):
                    last = nc.tensor.transpose(ps_y[:, j * P:(j + 1) * P], y[:, n % 2, j * P:(j + 1) * P], ident[:])
                last.then_inc(y_turned, 1)

            mixer_work = {"turn_x": turn_x, "project": project, "mix": mix, "turn_x1": turn_x1,
                          "logits": logits_of, "rank": rank, "hots": hots}
            for c in range(-1, CHUNKS):
                if c >= 0:
                    pe.wait_ge(experts_known, c + 1)
                if c == 0:
                    turn_weights()
                    pe.wait_ge(w_t_ready, 12)
                for t in range(TICKS):
                    for lag, work in ((1, up), (0, turn_rows), (3, down), (2, turn_y)):
                        if c >= 0 and 0 <= t - lag < MAX_BLOCKS:
                            work(c, t - lag)
                    run_parts(MIXER_PARTS, t, c + 1, mixer_work)

        @block.scalar
        def _(act):
            act.wait_ge(w_ready, 16 * 5)
            nc.scalar.activation(lam[:], lam_log[:], ACT.Sigmoid).then_inc(lam_ready, 1)

            def squares(c, _):
                act.wait_ge(x_loaded[c % 2], 16 * (c // 2 + 1))
                if c >= 1:
                    act.wait_ge(xn_ready, GROUPS * (c - 1) + 1)
                for i in range(TILES):
                    last = nc.scalar.activation(square_junk[:, i, :], x_in[:, c % 2, i, :], ACT.Square,
                                                accum_out=sumsq[:, i:i + 1])
                last.then_inc(sumsq_ready, 1)

            def copy_xn(c, g):
                n = GROUPS * c + g
                act.wait_ge(xn_turned, n + 1)
                if n >= 2:
                    act.wait_ge(proj_ready, 3 * (n - 1))
                nc.scalar.copy(x_norm_t[:, n % 2, :], ps_t[:]).then_inc(xn_t_ready, 1)

            def gates(c, g_k):
                g, k = g_k
                n = GROUPS * c + g
                m = 3 * n + k
                act.wait_ge(proj_ready, m + 1)
                if k < 2:
                    if c >= 1:
                        act.wait_ge(state_ready, n - GROUPS + 1)
                    nc.scalar.activation((tanh_a, tanh_r)[k][:, g, :], ps_p[m % 2][:], ACT.Tanh, scale=0.5
                                         ).then_inc(gates_ready, 1)
                else:
                    if n >= 2:
                        act.wait_ge(gelu_ready, n // 2)
                    nc.scalar.copy(value[:, g % 2, :], ps_p[m % 2][:]).then_inc(gates_ready, 1)

            def gelu(c, g):
                n = GROUPS * c + g
                act.wait_ge(gates_ready, 3 * (n + 2))
                if n >= 2:
                    act.wait_ge(state_ready, n)
                nc.scalar.activation(gelu_v[:].rearrange("p a b -> p (a b)"),
                                     value[:].rearrange("p a b -> p (a b)"), ACT.Gelu).then_inc(gelu_ready, 1)

            def x1_of(c, g):
                act.wait_ge(x1_stats, c + 1)
                if c >= 3 and g == 0:
                    act.wait_ge(x1_stored[c - 3], 16 * GROUPS)
                    act.wait_ge(s_done, GROUPS * (c - 2))
                for i in range(g * TPG, (g + 1) * TPG):
                    last = nc.scalar.activation(x1[c % 3][:, i, :], z[:, i, :], ACT.Identity,
                                                bias=neg_mean_rstd[:, i:i + 1], scale=rstd[:, i:i + 1])
                last.then_inc(x1_ready, 1)

            def copy_x1(c, g):
                n = GROUPS * c + g
                act.wait_ge(x1_turned, n + 1)
                if n >= 2:
                    act.wait_ge(logits_done, n - 1)
                nc.scalar.copy(x1_t[:, n % 2, :], ps_t[:]).then_inc(x1_t_ready, 1)

            def exps(c, _):
                act.wait_ge(shifted_ready, c + 1)
                nc.scalar.activation(exp_logits[c % 3][:], shifted[c % 2][:], ACT.Exp)
                nc.scalar.activation(exp_gap[c % 3][:], top_gap[c % 2][:], ACT.Exp).then_inc(exps_ready, 1)

            def copy_weights():
                w_v = w_t[:].rearrange("p (e n) -> p e n", n=W_STRIDE)
                for q in range(12):
                    act.wait_ge(w_turned, q + 1)
                    if q < 8:
                        nc.scalar.copy(w_v[:, q, 0:2 * INTER], ps_t[:]).then_inc(w_t_ready, 1)
                    else:
                        m = 2 * (q - 8)
                        nc.scalar.copy(w_v[:, m:m + 2, 2 * INTER:W_STRIDE],
                                       ps_t[:].rearrange("p (e k) -> p e k", e=2)).then_inc(w_t_ready, 1)

            def copy_rows(c, b):
                n = MAX_BLOCKS * c + b
                act.wait_ge(xg_turned, n + 1)
                nc.scalar.copy(xg_t[:, n % 2, :], ps_x[:, 0:P]).then_inc(xg_t_ready, 1)

            def gate(c, b):
                n = MAX_BLOCKS * c + b
                act.wait_ge(h_ready, n + 1)
                nc.scalar.activation(silu[:, n % 2, :], ps_h[n % 2][:, 0:INTER], ACT.Silu).then_inc(silu_ready, 1)

            def copy_y(c, b):
                n = MAX_BLOCKS * c + b
                act.wait_ge(y_turned, n + 1)
                nc.scalar.copy(y_t[:, n % 2, :], ps_y[:, 0:INTER]).then_inc(y_t_ready, 1)

            def copy_out(c, b):
                n = MAX_BLOCKS * c + b
                act.wait_ge(u_ready, n + 1)
                if n >= ROWS_RING:
                    act.wait_ge(rows_stored[n % ROWS_RING], 16 * uses_before(n, ROWS_RING))
                nc.scalar.copy(rows_out[:, n % ROWS_RING, :], ps_u[:, 0:D]).then_inc(rows_ready, 1)

            def out_of(c, g):
                act.wait_ge(out_stats, c + 1)
                if c >= 1 and g == 0:
                    act.wait_ge(out_stored[c - 1], 16 * GROUPS)
                for i in range(g * TPG, (g + 1) * TPG):
                    last = nc.scalar.activation(fin[:, i, :], s[:, i, :], ACT.Identity,
                                                bias=out_shift[:, i:i + 1], scale=out_rstd[:, i:i + 1])
                last.then_inc(fin_ready, 1)

            mixer_work = {"squares": squares, "turn_x": copy_xn, "project": gates, "gelu": gelu,
                          "x1": x1_of, "turn_x1": copy_x1, "slots": exps}
            for c in range(-1, CHUNKS + 1):
                if c == 0:
                    copy_weights()
                for t in range(TICKS):
                    for lag, work in ((1, gate), (0, copy_rows), (3, copy_out), (2, copy_y)):
                        if 0 <= c < CHUNKS and 0 <= t - lag < MAX_BLOCKS:
                            work(c, t - lag)
                    run_parts(MIXER_PARTS, t, c + 1, mixer_work)
                    run_parts(COMBINE_PARTS, t, c - 1, {"out": out_of})

        @block.vector
        def _(dve):
            steps = [0]

            def mark(ins):
                ins.then_inc(dve_step, 1)
                steps[0] += 1

            def after_marks():
                dve.wait_ge(dve_step, steps[0])

            def link(ins):
                mark(ins)
                after_marks()

            def inverse_root(dst, src, eps, scale):
                link(nc.vector.tensor_scalar(nr_half[:], src, scale, eps, ALU.mult, ALU.add))
                link(nc.vector.tensor_scalar(nr_int[:], nr_half[:].bitcast(I32), 1, None, ALU.arith_shift_right))
                link(nc.vector.tensor_scalar(dst.bitcast(I32), nr_int[:], -1.0, RSQRT_MAGIC, ALU.mult, ALU.add))
                link(nc.vector.tensor_scalar(nr_half[:], nr_half[:], -0.5, None, ALU.mult))
                for _ in range(3):
                    link(nc.vector.tensor_tensor(nr_tmp[:], dst, dst, ALU.mult))
                    link(nc.vector.tensor_tensor(nr_tmp[:], nr_tmp[:], nr_half[:], ALU.mult))
                    link(nc.vector.scalar_tensor_tensor(dst, nr_tmp[:], 1.5, dst, ALU.add, ALU.mult))

            def layer_stats(stats, rstd, shift):
                mark(nc.vector.tensor_tensor(mean[:], stats[:, :, 1], stats[:, :, 4], ALU.add))
                mark(nc.vector.tensor_tensor(mean_diff[:], stats[:, :, 1], stats[:, :, 4], ALU.subtract))
                mark(nc.vector.tensor_tensor(var[:], stats[:, :, 2], stats[:, :, 5], ALU.add))
                after_marks()
                link(nc.vector.tensor_tensor(mean_diff[:], mean_diff[:], mean_diff[:], ALU.mult))
                link(nc.vector.scalar_tensor_tensor(var[:], mean_diff[:], D / 4.0, var[:], ALU.mult, ALU.add))
                inverse_root(rstd[:], var[:], LN_EPS, 1.0 / D)
                return nc.vector.scalar_tensor_tensor(shift[:], mean[:], -0.5, rstd[:], ALU.mult, ALU.mult)

            def normalise(c, g):
                n = GROUPS * c + g
                if n >= 2:
                    dve.wait_ge(xn_turned, n - 1)
                tiles = slice(g * TPG, (g + 1) * TPG)
                nc.vector.tensor_tensor(x_norm[:, n % 2, :].rearrange("p (j d) -> p j d", j=TPG),
                                        x_in[:, c % 2, tiles, :],
                                        rms_inv[:, tiles].rearrange("p (j o) -> p j o", o=1).to_broadcast([P, TPG, D]),
                                        ALU.mult).then_inc(xn_ready, 1)

            def recur(c, g):
                n = GROUPS * c + g
                dve.wait_ge(gelu_ready, n // 2 + 1)
                if n >= 1:
                    dve.wait_ge(state_ready, n)
                mark(nc.vector.tensor_scalar(gate_a[:], tanh_a[:, g, :], 0.5, 0.5, ALU.mult, ALU.add))
                mark(nc.vector.scalar_tensor_tensor(u1[:], tanh_a[:, g, :], -1.0, gelu_v[:, g % 2, :],
                                                    ALU.add, ALU.mult))

            def scan(c, g):
                n = GROUPS * c + g
                after_marks()
                link(nc.vector.scalar_tensor_tensor(u2[:], tanh_r[:, g, :], 1.0, u1[:], ALU.add, ALU.mult))
                if n >= 2:
                    dve.wait_ge(mixed, n - 1)
                first = 0.0
                if g % SEQ_GROUPS:
                    first = state[:, (n - 1) % 2, GROUP - 1:GROUP]
                nc.vector.tensor_tensor_scan(state[:, n % 2, :], gate_a[:], u2[:], first, ALU.mult, ALU.add
                                             ).then_inc(state_ready, 1)

            def residual(c, g):
                n = GROUPS * c + g
                dve.wait_ge(mixed, n + 1)
                tiles = slice(g * TPG, (g + 1) * TPG)
                nc.vector.scalar_tensor_tensor(z[:, tiles, :].rearrange("p j d -> p (j d)"),
                                               x_in[:, c % 2, tiles, :].rearrange("p j d -> p (j d)"), 2.0,
                                               ps_t[:], ALU.mult, ALU.add).then_inc(z_ready, 1)
                dve.wait_ge(z_ready, n + 1)
                for i in range(g * TPG, (g + 1) * TPG):
                    mark(nc.vector.bn_stats(stats[:, i, :], z[:, i, :]))

            def rms(c, _):
                dve.wait_ge(sumsq_ready, c + 1)
                inverse_root(rms_inv[:], sumsq[:], RMS_EPS, 1.0 / D)

            def x1_statistics(c, _):
                after_marks()
                layer_stats(stats, rstd, neg_mean_rstd).then_inc(x1_stats, 1)

            def over_experts(v):
                return v.rearrange("p (i o) -> p i o", o=1).to_broadcast([P, TILES, E])

            def pick_top(k, values, top):
                link(nc.vector.tensor_reduce(top, values, AX.X, ALU.max))
                link(nc.vector.tensor_tensor(route_a[:], values, over_experts(top), ALU.is_equal))
                link(nc.vector.tensor_tensor(route_a[:], route_a[:], first_key[:], ALU.mult))
                link(nc.vector.tensor_reduce(route_b[:], route_a[:], AX.X, ALU.max))
                link(nc.vector.tensor_tensor(pick[:, k], first_key[:], over_experts(route_b[:]), ALU.is_equal))

            def pick_experts(c, k):
                if k == 0:
                    dve.wait_ge(logits_done, GROUPS * (c + 1))
                    nc.vector.tensor_copy(logits[:], ps_logits[:]).then_inc(logits_read, 1)
                    dve.wait_ge(logits_read, c + 1)
                    pick_top(0, logits[:], top1[:])
                    mark(nc.vector.tensor_tensor(shifted[c % 2][:], logits[:], over_experts(top1[:]), ALU.subtract))
                    after_marks()
                    link(nc.vector.scalar_tensor_tensor(logits[:], pick[:, 0], LOWEST, logits[:], ALU.mult, ALU.add))
                else:
                    pick_top(1, logits[:], top2[:])
                    nc.vector.tensor_tensor(picked[:, 0:TILES, :], pick[:, 0], pick[:, 1], ALU.add
                                            ).then_inc(picked_ready, 1)
                    nc.vector.tensor_tensor(top_gap[c % 2][:], top2[:], top1[:], ALU.subtract
                                            ).then_inc(shifted_ready, 1)

            def slots_of(c, _):
                dve.wait_ge(rank_ready, c + 1)
                link(nc.vector.tensor_scalar(count_i[:], ps_rank[:, TILES, :], float(P - 1), None, ALU.add))
                link(nc.vector.tensor_scalar(count_i[:], count_i[:], 7, None, ALU.arith_shift_right))
                link(nc.vector.tensor_copy(blocks_of[:], count_i[:]))
                link(nc.vector.tensor_tensor_scan(block_end[:], one_row[:], blocks_of[:], 0.0, ALU.mult, ALU.add))
                link(nc.vector.tensor_tensor(slot_base[:], block_end[:], blocks_of[:], ALU.subtract))
                link(nc.vector.tensor_scalar(slot_base[:], slot_base[:], float(P), None, ALU.mult))
                nc.vector.tensor_tensor(route_a[:], ps_rank[:, 0:TILES, :],
                                        slot_base[:].rearrange("p (o e) -> p o e", o=1).to_broadcast([P, TILES, E]),
                                        ALU.add).then_inc(rank_read, 1)
                dve.wait_ge(rank_read, c + 1)
                for k in range(2):
                    link(nc.vector.tensor_tensor(pick[:, k], pick[:, k], route_a[:], ALU.mult))
                    link(nc.vector.tensor_reduce(slot_f[:, k], pick[:, k], AX.X, ALU.add))
                slots = slot_i[c % 3]
                link(nc.vector.tensor_copy(slots[:], slot_f[:]))
                flat = slots[:].rearrange("p k i -> p (k i)")
                mark(nc.vector.tensor_scalar(part_i[:, 0], flat, 7, None, ALU.arith_shift_right))
                mark(nc.vector.tensor_scalar(part_i[:, 1], flat, P - 1, None, ALU.bitwise_and))
                after_marks()
                mark(nc.vector.tensor_copy(slot_block[:], part_i[:, 0]))
                mark(nc.vector.tensor_copy(slot_lane[:], part_i[:, 1]))
                after_marks()
            def block_experts(c, _):
                link(nc.vector.tensor_tensor(ended[:], block_no[:],
                                             block_end[:].rearrange("p (o e) -> p o e", o=1)
                                             .to_broadcast([P, MAX_BLOCKS, E]), ALU.is_ge))
                link(nc.vector.tensor_reduce(expert_f[:], ended[:], AX.X, ALU.add))
                link(nc.vector.tensor_scalar(expert_f[:], expert_f[:], float(E - 1), None, ALU.min))
                nc.vector.tensor_scalar(w_at[c % 2][:], expert_f[:], float(W_STRIDE), None, ALU.mult
                                        ).then_inc(experts_known, 1)

            def hots(c, q):
                for m in range(q * HOTS, (q + 1) * HOTS):
                    n = 2 * TILES * c + m
                    if n >= HOT_RING:
                        dve.wait_ge(hot_used, n - HOT_RING + 1)
                    nc.vector.tensor_scalar(lane_hot[:, m % HOT_RING, :], lane_iota[:], slot_lane[:, m:m + 1], None,
                                            ALU.is_equal)
                    nc.vector.scalar_tensor_tensor(block_hot[:, m % HOT_RING].rearrange("p a b -> p (a b)"),
                                                   block_iota[:].rearrange("p a b -> p (a b)"),
                                                   slot_block[:, m:m + 1],
                                                   token_parts[:, m % TILES].rearrange("p a b -> p (a b)"),
                                                   ALU.is_equal, ALU.mult).then_inc(hot_ready, 1)

            def token_lists(c, _):
                dve.wait_ge(hot_used, 2 * TILES * (c + 1))
                link(nc.vector.tensor_copy(token_ps[:], ps_token[:]))
                link(nc.vector.scalar_tensor_tensor(token_pj[:], token_ps[:, 0], float(TPG), token_ps[:, 1],
                                                    ALU.mult, ALU.add))
                if c >= 2:
                    for k in range(GATHER_RING):
                        dve.wait_ge(xg_ready[k], 16 * filled(c - 2, GATHER_RING, k))
                nc.vector.scalar_tensor_tensor(token_of[c % 2][:], token_ps[:, 2], float(GROUP), token_pj[:],
                                               ALU.mult, ALU.add).then_inc(tokens_known, 1)

            def product(c, b):
                n = MAX_BLOCKS * c + b
                dve.wait_ge(silu_ready, n + 1)
                nc.vector.tensor_tensor(y[:, n % 2, :], silu[:, n % 2, :], ps_h[n % 2][:, INTER:2 * INTER],
                                        ALU.mult).then_inc(y_ready, 1)

            def weights(c, _):
                dve.wait_ge(exps_ready, c + 1)
                link(nc.vector.tensor_reduce(route_b[:], exp_logits[c % 3][:], AX.X, ALU.add))
                link(nc.vector.reciprocal(weight[:, 0], route_b[:]))
                link(nc.vector.tensor_tensor(weight[:, 1], weight[:, 0], exp_gap[c % 3][:], ALU.mult))

            def combine_first(c, g):
                dve.wait_ge(og_ready[g], 16 * 2 * TPG * (c + 1))
                if c >= 1 and g == 0:
                    dve.wait_ge(fin_ready, GROUPS * c)
                for i in range(g * TPG, (g + 1) * TPG):
                    mark(nc.vector.scalar_tensor_tensor(s[:, i, :], og[:, 0, i, :], weight[:, 0, i:i + 1],
                                                        x1[c % 3][:, i, :], ALU.mult, ALU.add))

            def combine_second(c, g):
                after_marks()
                for i in range(g * TPG, (g + 1) * TPG):
                    last = nc.vector.scalar_tensor_tensor(s[:, i, :], og[:, 1, i, :], weight[:, 1, i:i + 1],
                                                          s[:, i, :], ALU.mult, ALU.add)
                last.then_inc(s_done, 1)
                dve.wait_ge(s_done, GROUPS * c + g + 1)
                for i in range(g * TPG, (g + 1) * TPG):
                    mark(nc.vector.bn_stats(out_bn[:, i, :], s[:, i, :]))

            def out_statistics(c, _):
                after_marks()
                layer_stats(out_bn, out_rstd, out_shift).then_inc(out_stats, 1)

            dve.wait_ge(w_ready, 16 * 5)
            dve.wait_ge(consts_ready, CONSTS)
            dve.wait_ge(lam_ready, 1)
            mark(nc.vector.tensor_scalar(w_in_sb[:], w_in_raw[:], w_norm_sb[:], None, ALU.mult))
            mark(nc.vector.tensor_scalar(w_out_sb[:], w_out_raw[:], lam[:], -0.25, ALU.mult, ALU.mult))
            after_marks()
            mixer_work = {"rms": rms, "normalise": normalise, "recur": recur, "scan": scan, "residual": residual,
                          "x1_stats": x1_statistics, "pick": pick_experts, "slots": slots_of,
                          "block_experts": block_experts, "hots": hots, "token_lists": token_lists}
            combine_work = {"weights": weights, "first": combine_first, "second": combine_second,
                            "out_stats": out_statistics}
            for c in range(-1, CHUNKS + 1):
                for t in range(TICKS):
                    if 0 <= c < CHUNKS and 0 <= t - 1 < MAX_BLOCKS:
                        product(c, t - 1)
                    run_parts(MIXER_PARTS, t, c + 1, mixer_work)
                    run_parts(COMBINE_PARTS, t, c - 1, combine_work)


_INS = ["L0_attn_x", "L0_attn_w_norm", "L0_attn_W_in", "L0_attn_lambda_log", "L0_attn_W_out",
        "L0_ffn_w1", "L0_ffn_w2", "L0_ffn_router_w"]


def kernel(**inputs):
    import numpy as _np
    import concourse.bacc as _bacc
    from concourse import mybir as _mybir
    from concourse.bass_utils import run_bass_kernel_spmd as _run

    nc = _bacc.Bacc("TRN2", target_bir_lowering=False, num_devices=1)
    arrays, args = {}, []
    for name in _INS:
        a = _np.ascontiguousarray(inputs[name])
        arrays[f"in_{name}"] = a
        args.append(nc.dram_tensor(f"in_{name}", a.shape, _mybir.dt.from_np(a.dtype), kind="ExternalInput").ap())
    out = nc.dram_tensor("out", (8, 1024, 128), _mybir.dt.from_np(_np.dtype("float32")), kind="ExternalOutput").ap()
    moe_layer(nc, *args, out)
    r = _run(nc, [arrays], core_ids=[0])
    return r.results[0]["out"]
```

```python
import concourse.bass as bass
from concourse import mybir
from contextlib import ExitStack

F32 = mybir.dt.float32
BF16 = mybir.dt.bfloat16
I32 = mybir.dt.int32
ALU = mybir.AluOpType
ACT = mybir.ActivationFunctionType
AX = mybir.AxisListType

P = 128
D = 128
E = 8
INTER = 256
SEQ = 1024
GROUP = 512
TPG = GROUP // P
SEQ_GROUPS = SEQ // GROUP
CHUNK_SEQS = (1, 2, 2, 2, 1)
CHUNKS = len(CHUNK_SEQS)
GROUPS = [SEQ_GROUPS * q for q in CHUNK_SEQS]
TILES = [TPG * g for g in GROUPS]
BLOCKS = [2 * t + E - 1 for t in TILES]
FIRST_GROUP = [sum(GROUPS[:c]) for c in range(CHUNKS + 1)]
FIRST_BLOCK = [sum(BLOCKS[:c]) for c in range(CHUNKS + 1)]
ALL_BLOCKS = FIRST_BLOCK[CHUNKS]
GELU_GROUPS = [SEQ_GROUPS, SEQ_GROUPS] + [max(GROUPS)] * (CHUNKS - 2)
MAX_GROUPS, MAX_TILES, MAX_BLOCKS = max(GROUPS), max(TILES), max(BLOCKS)
ROWS_RING = 4
GATHER_RING = 16
W_STRIDE = 2 * INTER + 2 * D
W_TURNS = 12
XT_RING = 3
HOTS = 2
HOT_RING = 8

RMS_EPS = 1e-6
LN_EPS = 1e-5
LOWEST = -3.0e38
RSQRT_MAGIC = float(0x5F3759DF)


TIMETABLE = {
    "squares": (
        (-89, -88, -87, -86),
        (-61, -59, -59, -58, -55, -54, -54, -53),
        (-47, -41, -34, -30, -29, -26, -24, -18),
        (0, 3, 6, 6, 6, 7, 7, 20),
        (33, 46, 48, 58),
    ),
    "rms": (
        (-85, -84),
        (-51, -50),
        (-16, -16),
        (22, 25),
        (64, 70),
    ),
    "normalise": (
        (-83, -82),
        (-49, -42, -38, -29),
        (-11, -10, -1, -1),
        (27, 31, 40, 40),
        (75, 83),
    ),
    "turn_x": (
        (-81, -80),
        (-44, -37, -29, -23),
        (-10, -5, 1, 5),
        (28, 34, 41, 43),
        (76, 85),
    ),
    "project": (
        (-79, -79, -78, -77, -76, -76),
        (-40, -36, -31, -28, -27, -26, -25, -23, -22, -19, -16, -15),
        (-8, -7, -7, -2, -2, 0, 2, 5, 6, 7, 8, 9),
        (29, 30, 32, 35, 38, 40, 42, 43, 44, 45, 47, 48),
        (78, 81, 82, 86, 87, 91),
    ),
    "gelu": (
        (-75,),
        (-26, -15),
        (10,),
        (49,),
        (96,),
    ),
    "recur": (
        (-74, -71),
        (-26, -22, -11, -10),
        (10, 12, 17, 21),
        (49, 51, 54, 60),
        (97, 99),
    ),
    "scan": (
        (-72, -68),
        (-23, -20, -11, -9),
        (10, 13, 20, 23),
        (50, 53, 58, 63),
        (98, 100),
    ),
    "turn_weights": (
        (-44, -35, -33, -27, -26, -25, -19, -15, -12, -11, -6, -5),
    ),
    "mix": (
        (-70, -65),
        (-20, -14, -10, -8),
        (13, 15, 21, 25),
        (52, 55, 60, 64),
        (100, 103),
    ),
    "residual": (
        (-67, -64),
        (-20, -13, -10, -6),
        (13, 16, 24, 26),
        (52, 57, 62, 64),
        (101, 103),
    ),
    "x1_stats": (
        (-62, -60),
        (-4, -4),
        (28, 29),
        (64, 66),
        (107, 108),
    ),
    "x1": (
        (-57, -56, -52, -45),
        (-4, -4, -4, -3, 0, 1, 3, 3),
        (30, 30, 30, 30, 31, 31, 31, 31),
        (67, 68, 69, 69, 71, 71, 72, 73),
        (108, 110, 110, 111),
    ),
    "turn_x1": (
        (-48, -43),
        (-2, 0, 3, 4),
        (31, 32, 33, 35),
        (69, 70, 73, 74),
        (112, 113),
    ),
    "logits": (
        (-46, -39),
        (0, 2, 4, 4),
        (32, 34, 36, 37),
        (70, 72, 75, 75),
        (113, 115),
    ),
    "pick": (
        (-32, -31),
        (4, 5),
        (37, 39),
        (75, 77),
        (115, 115),
    ),
    "rank": (
        (-28,),
        (6,),
        (41,),
        (80,),
        (115,),
    ),
    "slots": (
        (-28, -28),
        (6, 7),
        (41, 42),
        (81, 82),
        (115, 116),
    ),
    "hots": (
        (-28, -27, -26, -23, -23, -20, -19, -16),
        (7, 8, 8, 9, 9, 9, 9, 9, 11, 11, 13, 14, 14, 14, 14, 15),
        (43, 43, 44, 44, 45, 46, 47, 47, 47, 48, 48, 48, 48, 48, 48, 49),
        (85, 86, 87, 87, 89, 89, 90, 90, 90, 90, 90, 91, 92, 93, 93, 94),
        (116, 116, 119, 119, 121, 123, 124, 124),
    ),
    "hot_sums": (
        (-23, -21, -19, -19, -17, -11, -11, -11),
        (10, 10, 10, 10, 10, 10, 10, 13, 14, 14, 15, 15, 15, 15, 17, 17),
        (44, 45, 45, 46, 46, 47, 48, 49, 49, 49, 49, 49, 49, 50, 53, 56),
        (86, 89, 90, 90, 90, 91, 91, 91, 91, 92, 93, 93, 93, 95, 95, 95),
        (117, 118, 120, 123, 123, 125, 127, 127),
    ),
    "exps": (
        (-9,),
        (14,),
        (64,),
        (90,),
        (170,),
    ),
    "block_experts": (
        (-2,),
        (20,),
        (42,),
        (84,),
        (138,),
    ),
    "token_lists": (
        (-5,),
        (18,),
        (56,),
        (95,),
        (127,),
    ),
    "weights": (
        (33,),
        (74,),
        (115,),
        (162,),
        (188,),
    ),
    "first": (
        (35, 44),
        (79, 81, 98, 102),
        (134, 137, 141, 148),
        (169, 171, 172, 178),
        (189, 191),
    ),
    "second": (
        (35, 45),
        (85, 86, 102, 105),
        (136, 146, 146, 156),
        (173, 175, 177, 179),
        (189, 192),
    ),
    "out_bn": (
        (40, 51),
        (95, 104, 104, 105),
        (145, 153, 155, 157),
        (174, 176, 180, 181),
        (190, 193),
    ),
    "out_stats": (
        (55, 59),
        (113, 113),
        (159, 160),
        (181, 182),
        (194, 195),
    ),
    "out": (
        (69, 72, 73, 73),
        (114, 114, 117, 119, 122, 127, 127, 131),
        (160, 161, 162, 162, 165, 166, 167, 168),
        (183, 183, 184, 185, 186, 186, 186, 187),
        (196, 197, 198, 199),
    ),
    "results": (
        (32, 32, 36, 36, 37, 37, 37, 37, 43, 46, 46, 46, 47, 47, 49, 50),
        (75, 75, 77, 77, 77, 77, 79, 79, 79, 84, 84, 84, 86, 86, 86, 86, 88, 91, 91, 97, 97, 98, 98, 98, 98, 98, 99,
         99, 99, 100, 100, 100),
        (120, 120, 121, 121, 121, 121, 126, 126, 126, 126, 126, 126, 126, 129, 129, 129, 129, 129, 131, 131, 134,
         134, 134, 137, 137, 137, 137, 143, 145, 149, 152, 158),
        (160, 160, 160, 160, 160, 160, 160, 160, 160, 163, 163, 163, 163, 163, 163, 163, 163, 163, 163, 163, 163,
         163, 163, 163, 163, 163, 163, 163, 163, 163, 163, 163),
        (163, 163, 163, 163, 163, 163, 163, 163, 163, 163, 163, 163, 163, 163, 163, 163),
    ),
    "input_u": (
        (-73, -69),
        (-24, -21, -11, -10),
        (10, 12, 19, 22),
        (49, 52, 54, 62),
        (97, 100),
    ),
    "z_bn": (
        (-66, -63),
        (-9, -9, -9, -4),
        (16, 18, 24, 27),
        (57, 61, 63, 64),
        (101, 104),
    ),
}

PART_ORDER = ("squares", "rms", "turn_x", "project", "normalise", "gelu", "mix", "recur", "input_u", "residual", "scan",
              "z_bn",              "x1_stats", "x1", "turn_x1", "logits", "pick", "exps", "rank", "slots", "hots", "hot_sums",
              "block_experts", "token_lists", "weights", "first", "second", "out_bn", "out_stats", "out",
              "turn_weights")


def part_args(name, c):
    counts = {"rms": 2, "x1_stats": 2, "pick": 2, "slots": 2, "out_stats": 2, "gelu": -(-GROUPS[c] // GELU_GROUPS[c]),
              "project": 3 * GROUPS[c], "squares": 2 * GROUPS[c], "x1": 2 * GROUPS[c], "out": 2 * GROUPS[c],
              "hots": 2 * TILES[c] // HOTS, "hot_sums": 2 * TILES[c] // HOTS, "turn_weights": W_TURNS}
    for name_of_group in ("normalise", "turn_x", "mix", "recur", "input_u", "scan", "z_bn", "residual", "turn_x1", "logits", "first",
                          "second", "out_bn"):
        counts[name_of_group] = GROUPS[c]
    args = range(counts.get(name, 1))
    if name == "gelu":
        return [GELU_GROUPS[c] * k for k in args]
    return [divmod(k, 3) for k in args] if name == "project" else list(args)


def schedule():
    ticks = {}
    for name in PART_ORDER:
        for c in reversed(range(CHUNKS)):
            if c < len(TIMETABLE[name]):
                for t, arg in zip(TIMETABLE[name][c], part_args(name, c), strict=True):
                    ticks.setdefault(t, []).append((name, c, arg))
    return min(ticks), max(max(ticks) + 1, ALL_BLOCKS + 3), ticks


FIRST_TICK, END_TICK, SCHEDULE = schedule()

BANK_T_USES = [part for t in range(FIRST_TICK, END_TICK) for part in SCHEDULE.get(t, ())
               if part[0] in ("turn_x", "turn_x1", "mix")]
TURNS = [part for part in BANK_T_USES if part[0] != "mix"]


def run_parts(tick, work):
    for name, c, arg in SCHEDULE.get(tick, ()):
        if name in work:
            work[name](c, arg)


def run_blocks(tick, lags):
    for lag, work in lags:
        n = tick - lag
        if 0 <= n < ALL_BLOCKS:
            c = max(c for c in range(CHUNKS) if FIRST_BLOCK[c] <= n)
            work(c, n - FIRST_BLOCK[c], n)


def moe_layer(nc, x, w_norm, w_in, lambda_log, w_out, w1, w2, router_w, out):
    x_rows = x.rearrange("b t d -> (b t) d")
    out_rows = out.rearrange("b t d -> (b t) d")

    def group_view(rows, g):
        r0 = g * GROUP
        return rows[r0:r0 + GROUP, :].rearrange("(p j) d -> p (j d)", j=TPG)

    x1_dram = [nc.dram_tensor(f"x1_rows_{c}", [GROUP * GROUPS[c], D], F32, kind="Internal").ap() for c in range(CHUNKS)]
    slot_dram = [nc.dram_tensor(f"slot_rows_{c}", [BLOCKS[c] * P, D], F32, kind="Internal").ap()
                 for c in range(CHUNKS)]

    with ExitStack() as ctx:
        def sb(name, shape, dt=F32):
            return ctx.enter_context(nc.sbuf_tensor(name, shape, dt))

        def bank(name):
            return ctx.enter_context(nc.psum_tensor(name, [P, 512], F32))

        def sem(name):
            return ctx.enter_context(nc.semaphore(name))

        w_in_raw = sb("w_in_raw", [P, 3 * D])
        w_in_sb = sb("w_in_sb", [P, 3 * D])
        w_out_sb = sb("w_out_sb", [P, D])
        w_norm_sb = sb("w_norm_sb", [P, 1])
        lam_log = sb("lam_log", [P, 1])
        lam = sb("lam", [P, 1])
        w_out_raw = sb("w_out_raw", [P, D])
        router_t = sb("router_t", [P, E])
        w_t = sb("w_t", [P, E * W_STRIDE])
        ident = sb("ident", [P, P])
        before = sb("before", [P, P], BF16)
        ones = sb("ones", [P, P], BF16)
        lane_iota = sb("lane_iota", [P, P], BF16)
        block_iota = sb("block_iota", [P, 2, MAX_BLOCKS], BF16)
        token_parts = sb("token_parts", [P, MAX_TILES, 2, MAX_BLOCKS], BF16)
        first_key = sb("first_key", [P, MAX_TILES, E])
        block_no = sb("block_no", [P, MAX_BLOCKS, E])

        x_in = sb("x_in", [P, 2, MAX_TILES, D])
        square_junk = sb("square_junk", [P, MAX_TILES, D])
        sumsq = sb("sumsq", [P, MAX_TILES])
        rms_inv = sb("rms_inv", [P, MAX_TILES])
        nr_half, nr_tmp = ([sb(f"{name}_{k}", [P, MAX_TILES]) for k in range(3)] for name in ("nr_half", "nr_tmp"))
        nr_int = [sb(f"nr_int_{k}", [P, MAX_TILES], I32) for k in range(3)]
        x_norm = sb("x_norm", [P, 2, GROUP])
        x_norm_t = sb("x_norm_t", [P, 2, GROUP])
        tanh_a = sb("tanh_a", [P, MAX_GROUPS, GROUP])
        tanh_r = sb("tanh_r", [P, MAX_GROUPS, GROUP])
        value = sb("value", [P, MAX_GROUPS, GROUP])
        gate_a = sb("gate_a", [P, GROUP])
        u1 = sb("u1", [P, GROUP])
        u2 = sb("u2", [P, GROUP])
        state = sb("state", [P, 2, GROUP])
        z = sb("z", [P, MAX_TILES, D])
        stats = sb("stats", [P, MAX_TILES, 6])
        mean = [sb(f"mean_{k}", [P, MAX_TILES]) for k in range(2)]
        mean_diff = [sb(f"mean_diff_{k}", [P, MAX_TILES]) for k in range(2)]
        var = [sb(f"var_{k}", [P, MAX_TILES]) for k in range(2)]
        rstd = sb("rstd", [P, MAX_TILES])
        neg_mean_rstd = sb("neg_mean_rstd", [P, MAX_TILES])
        x1 = [sb(f"x1_{k}", [P, MAX_TILES, D]) for k in range(3)]
        x1_t = sb("x1_t", [P, 2, GROUP])

        logits = sb("logits", [P, MAX_TILES, E])
        top1 = sb("top1", [P, MAX_TILES])
        top2 = sb("top2", [P, MAX_TILES])
        top_gap = [sb(f"top_gap_{k}", [P, MAX_TILES]) for k in range(2)]
        route_a = sb("route_a", [P, MAX_TILES, E])
        route_b = sb("route_b", [P, MAX_TILES])
        pick = sb("pick", [P, 2, MAX_TILES, E])
        picked = {tiles: sb(f"picked_{tiles}", [P, tiles + 1, E], BF16) for tiles in sorted(set(TILES))}
        shifted = [sb(f"shifted_{k}", [P, MAX_TILES, E]) for k in range(2)]
        exp_logits = [sb(f"exp_logits_{k}", [P, MAX_TILES, E]) for k in range(3)]
        exp_gap = [sb(f"exp_gap_{k}", [P, MAX_TILES]) for k in range(3)]
        exp_sum = sb("exp_sum", [P, MAX_TILES])
        weight = sb("weight", [P, 2, MAX_TILES])
        count_i = sb("count_i", [P, E], I32)
        blocks_of = sb("blocks_of", [P, E])
        block_end = sb("block_end", [P, E])
        slot_base = sb("slot_base", [P, E])
        one_row = sb("one_row", [P, E])
        slot_f = sb("slot_f", [P, 2, MAX_TILES])
        slot_i = [sb(f"slot_i_{k}", [P, 2, MAX_TILES], I32) for k in range(3)]
        part_i = sb("part_i", [P, 2, 2, MAX_TILES], I32)
        slot_block = sb("slot_block", [P, 2, MAX_TILES])
        slot_lane = sb("slot_lane", [P, 2, MAX_TILES])
        ended = sb("ended", [P, MAX_BLOCKS, E])
        expert_f = sb("expert_f", [P, MAX_BLOCKS])
        w_at = [sb(f"w_at_{k}", [P, MAX_BLOCKS], I32) for k in range(2)]
        lane_hot = sb("lane_hot", [P, HOT_RING, P], BF16)
        block_hot = sb("block_hot", [P, HOT_RING, 2, MAX_BLOCKS], BF16)
        token_at = sb("token_at", [P, 2, MAX_BLOCKS], I32)
        tile_parts = sb("tile_parts", [P, 2, MAX_BLOCKS], I32)
        token_pj = sb("token_pj", [P, MAX_BLOCKS])
        token_of = [sb(f"token_of_{k}", [P, MAX_BLOCKS], I32) for k in range(2)]

        xg = [sb(f"xg_{k}", [P, D]) for k in range(GATHER_RING)]
        xg_t = sb("xg_t", [P, XT_RING, P])
        w_up = sb("w_up", [P, 2, 2 * INTER])
        silu = sb("silu", [P, 2, INTER])
        y = sb("y", [P, 2, INTER])
        rows_out = sb("rows_out", [P, ROWS_RING, D])

        og = sb("og", [P, 2, MAX_TILES, D])
        s = sb("s", [P, MAX_TILES, D])
        out_bn = sb("out_bn", [P, MAX_TILES, 6])
        out_rstd = sb("out_rstd", [P, MAX_TILES])
        out_shift = sb("out_shift", [P, MAX_TILES])
        fin = sb("fin", [P, MAX_TILES, D])
        w1_raw = og[:].rearrange("p k i d -> p (k i) d")
        w2_raw = s

        ps_t = bank("ps_t")
        ps_p = bank("ps_p")
        ps_q = bank("ps_q")
        ps_h = [bank("ps_h0"), bank("ps_h1")]
        ps_x = [bank("ps_x0"), bank("ps_x1")]
        ps_u = bank("ps_u")
        ps_rank = ps_q[:, 0:(MAX_TILES + 1) * E].rearrange("p (i e) -> p i e", e=E)
        ps_logits = ps_rank[:, 0:MAX_TILES, :]
        ps_token = ps_q[:, 0:2 * MAX_BLOCKS].rearrange("p (a b) -> p a b", a=2)

        w_ready = sem("w_ready")
        experts_in = sem("experts_in")
        consts_ready = sem("consts_ready")
        consts_step = sem("consts_step")
        lam_ready = sem("lam_ready")
        x_loaded = [sem(f"x_loaded_{c}") for c in range(CHUNKS)]
        sumsq_ready = sem("sumsq_ready")
        xn_ready = sem("xn_ready")
        turned = sem("turned")
        turn_copied = sem("turn_copied")
        proj_ready = sem("proj_ready")
        gates_ready = sem("gates_ready")
        gelu_ready = sem("gelu_ready")
        state_ready = sem("state_ready")
        mixed = sem("mixed")
        z_ready = sem("z_ready")
        x1_stats = sem("x1_stats")
        x1_ready = sem("x1_ready")
        x1_stored = [sem(f"x1_stored_{c}") for c in range(CHUNKS)]
        logits_done = sem("logits_done")
        logits_read = sem("logits_read")
        shifted_ready = sem("shifted_ready")
        exps_ready = sem("exps_ready")
        picked_ready = sem("picked_ready")
        rank_ready = sem("rank_ready")
        experts_known = sem("experts_known")
        hot_ready = sem("hot_ready")
        hot_used = sem("hot_used")
        tokens_known = sem("tokens_known")
        w_turned = sem("w_turned")
        w_t_ready = sem("w_t_ready")
        xg_ready = [sem(f"xg_ready_{k}") for k in range(GATHER_RING)]
        xg_turned = sem("xg_turned")
        xg_t_ready = sem("xg_t_ready")
        w_up_ready = sem("w_up_ready")
        h_ready = sem("h_ready")
        silu_ready = sem("silu_ready")
        y_ready = sem("y_ready")
        u_ready = sem("u_ready")
        rows_ready = sem("rows_ready")
        rank_read = sem("rank_read")
        rows_stored = [sem(f"rows_stored_{k}") for k in range(ROWS_RING)]
        og_ready = [sem(f"og_ready_{g}") for g in range(MAX_GROUPS)]
        s_done = sem("s_done")
        out_stats = sem("out_stats")
        fin_ready = sem("fin_ready")
        out_stored = [sem(f"out_stored_{c}") for c in range(CHUNKS)]
        dve_step = sem("dve_step")

        def half_group(h):
            return range(h * TPG // 2, (h + 1) * TPG // 2)

        def fills(ring, k, blocks):
            return (blocks - k + ring - 1) // ring

        def og_fills(c, g):
            return 16 * 2 * TPG * sum(g < GROUPS[h] for h in range(c))

        def project_bank(c, k):
            return (ps_p, ps_h[0], ps_h[1])[k] if c == 0 else ps_p

        def w_bank(q):
            return ps_x[q % 2]

        block = ctx.enter_context(nc.Block())

        @block.sync
        def _(sp):
            def load_x(c):
                if c >= 2:
                    sp.wait_ge(z_ready, FIRST_GROUP[c - 1])
                for g in range(GROUPS[c]):
                    sp.dma_start(x_in[:, c % 2, g * TPG:(g + 1) * TPG, :].rearrange("p j d -> p (j d)"),
                                 group_view(x_rows, FIRST_GROUP[c] + g)).then_inc(x_loaded[c], 16)

            def next_x(c, g):
                if g == GROUPS[c] - 1 and c + 2 < CHUNKS:
                    load_x(c + 2)

            def store_x1(c, h):
                g = h // 2
                if h % 2 == 0:
                    return
                sp.wait_ge(x1_ready, 2 * (FIRST_GROUP[c] + g + 1))
                sp.dma_start(group_view(x1_dram[c], g),
                             x1[c % 3][:, g * TPG:(g + 1) * TPG, :].rearrange("p j d -> p (j d)")
                             ).then_inc(x1_stored[c], 16)

            def store_block(c, b, n):
                sp.wait_ge(rows_ready, n + 1)
                sp.dma_start(slot_dram[c][b * P:(b + 1) * P, :], rows_out[:, n % ROWS_RING, :]
                             ).then_inc(rows_stored[n % ROWS_RING], 16)

            def store_out(c, h):
                g = h // 2
                if h % 2 == 0:
                    return
                sp.wait_ge(fin_ready, 2 * (FIRST_GROUP[c] + g + 1))
                sp.dma_start(group_view(out_rows, FIRST_GROUP[c] + g),
                             fin[:, g * TPG:(g + 1) * TPG, :].rearrange("p j d -> p (j d)")
                             ).then_inc(out_stored[c], 16)

            load_x(0)
            with nc.allow_non_contiguous_dma(reason="the router's 1024 weights, once"):
                sp.dma_start(router_t[:], router_w.rearrange("e d -> d e")).then_inc(w_ready, 16)
            sp.dma_start(w_in_raw[:], w_in).then_inc(w_ready, 16)
            sp.dma_start(w_norm_sb[:], w_norm.rearrange("(d o) -> d o", o=1)).then_inc(w_ready, 16)
            sp.dma_start(lam_log[:], lambda_log.rearrange("(d o) -> d o", o=1)).then_inc(w_ready, 16)
            sp.dma_start(w_out_raw[:], w_out).then_inc(w_ready, 16)
            load_x(1)
            sp.dma_start(w1_raw, w1.rearrange("e (k p) d -> p (e k) d", p=P)).then_inc(experts_in, 16)
            sp.dma_start(w2_raw[:].rearrange("p (e k) i -> p e (k i)", k=2), w2.rearrange("e p i -> p e i")
                         ).then_inc(experts_in, 16)
            for t in range(FIRST_TICK, END_TICK):
                run_blocks(t, ((3, store_block),))
                run_parts(t, {"residual": next_x, "x1": store_x1, "out": store_out})
            for c in range(CHUNKS):
                sp.wait_ge(out_stored[c], 16 * GROUPS[c])

        @block.gpsimd
        def _(gp):
            nc.gpsimd.memset(ident[:], 0.0).then_inc(consts_step, 1)
            nc.gpsimd.memset(before[:], 1.0).then_inc(consts_step, 1)
            gp.wait_ge(consts_step, 2)
            nc.gpsimd.affine_select(out=ident[:], in_=ident[:], compare_op=ALU.not_equal, fill=1.0, base=0,
                                    pattern=[[-1, P]], channel_multiplier=1).then_inc(consts_ready, 1)
            nc.gpsimd.affine_select(out=before[:], in_=before[:], compare_op=ALU.is_gt, fill=0.0, base=0,
                                    pattern=[[1, P]], channel_multiplier=-1).then_inc(consts_ready, 1)
            nc.gpsimd.memset(ones[:], 1.0).then_inc(consts_ready, 1)
            nc.gpsimd.memset(one_row[:], 1.0).then_inc(consts_ready, 1)
            for rows in picked.values():
                nc.gpsimd.memset(rows[:], 0.0).then_inc(consts_ready, 1)
            small = dict(allow_small_or_imprecise_dtypes=True)
            nc.gpsimd.iota(lane_iota[:], pattern=[[1, P]], base=0, channel_multiplier=0, **small).then_inc(consts_ready, 1)
            nc.gpsimd.iota(block_iota[:], pattern=[[0, 2], [1, MAX_BLOCKS]], base=0, channel_multiplier=0,
                           **small).then_inc(consts_ready, 1)
            nc.gpsimd.iota(token_parts[:, :, 0, :], pattern=[[0, MAX_TILES], [0, MAX_BLOCKS]], base=0,
                           channel_multiplier=1, **small).then_inc(consts_ready, 1)
            nc.gpsimd.iota(token_parts[:, :, 1, :], pattern=[[1, MAX_TILES], [0, MAX_BLOCKS]], base=0,
                           channel_multiplier=0, **small).then_inc(consts_ready, 1)
            nc.gpsimd.iota(first_key[:], pattern=[[0, MAX_TILES], [-1, E]], base=E, channel_multiplier=0,
                           **small).then_inc(consts_ready, 1)
            nc.gpsimd.iota(block_no[:], pattern=[[1, MAX_BLOCKS], [0, E]], base=0, channel_multiplier=0,
                           **small).then_inc(consts_ready, 1)

            def gather_block(c, b, n):
                if b == 0:
                    gp.wait_ge(x1_stored[c], 16 * GROUPS[c])
                    gp.wait_ge(tokens_known, c + 1)
                if n >= GATHER_RING:
                    gp.wait_ge(xg_turned, n - GATHER_RING + 1)
                gp.indirect_dma_start(xg[n % GATHER_RING][:], None, x1_dram[c],
                                      bass.IndirectOffsetOnAxis(ap=token_of[c % 2][:, b:b + 1], axis=0)
                                      ).then_inc(xg_ready[n % GATHER_RING], 16)

            def gather_result(c, m):
                k, i = m % 2, m // 2
                if m == 0:
                    for place in range(ROWS_RING):
                        gp.wait_ge(rows_stored[place], 16 * fills(ROWS_RING, place, FIRST_BLOCK[c + 1]))
                if c >= 1 and m % (2 * TPG) == 0:
                    gp.wait_ge(s_done, FIRST_GROUP[c - 1] + min(m // (2 * TPG) + 1, GROUPS[c - 1]))
                gp.indirect_dma_start(og[:, k, i, :], None, slot_dram[c],
                                      bass.IndirectOffsetOnAxis(ap=slot_i[c % 3][:, k, i:i + 1], axis=0)
                                      ).then_inc(og_ready[i // TPG], 16)

            for c in range(CHUNKS):
                for b in range(BLOCKS[c]):
                    n = FIRST_BLOCK[c] + b
                    gather_block(c, b, n)
                    for h in range(CHUNKS):
                        for m, after in enumerate(TIMETABLE["results"][h]):
                            if after == n:
                                gather_result(h, m)
            for h in range(CHUNKS):
                for m, after in enumerate(TIMETABLE["results"][h]):
                    if after >= ALL_BLOCKS:
                        gather_result(h, m)

        PE, ACT_ENGINE = mybir.EngineType.PE, mybir.EngineType.Activation
        CONSTS = 10 + len(picked)

        @block.tensor
        def _(pe):
            pe.wait_ge(consts_ready, CONSTS)
            pe.wait_ge(w_ready, 16 * 5)

            def free_bank_t(part):
                at = BANK_T_USES.index(part)
                if at and BANK_T_USES[at - 1][0] == "mix":
                    pe.wait_ge(z_ready, sum(use[0] == "mix" for use in BANK_T_USES[:at]))
                elif at:
                    pe.wait_ge(turn_copied, sum(use[0] != "mix" for use in BANK_T_USES[:at]))

            def turn_x(c, g):
                n = FIRST_GROUP[c] + g
                pe.wait_ge(xn_ready, n + 1)
                free_bank_t(("turn_x", c, g))
                t = ps_t[:].rearrange("p (q j) -> p j q", j=TPG)
                for j in range(TPG):
                    last = nc.tensor.transpose(t[:, j, :], x_norm[:, n % 2, j * D:(j + 1) * D], ident[:])
                last.then_inc(turned, 1)

            def project(c, g_k):
                g, k = g_k
                n = FIRST_GROUP[c] + g
                m = 3 * n + k
                if k == 0:
                    pe.wait_ge(turn_copied, TURNS.index(("turn_x", c, g)) + 1)
                if c >= 1:
                    pe.wait_ge(gates_ready, m)
                elif m >= 3:
                    pe.wait_ge(gates_ready, m - 2)
                nc.tensor.matmul(project_bank(c, k)[:], w_in_sb[:, k * D:(k + 1) * D], x_norm_t[:, n % 2, :],
                                 start=True, stop=True).then_inc(proj_ready, 1)

            def mix(c, g):
                n = FIRST_GROUP[c] + g
                pe.wait_ge(state_ready, n + 1)
                free_bank_t(("mix", c, g))
                st = state[:, n % 2, :].rearrange("p (q j) -> p j q", j=TPG)
                for j in range(TPG):
                    last = nc.tensor.matmul(ps_t[:, j * D:(j + 1) * D], st[:, j, :], w_out_sb[:],
                                            start=True, stop=True)
                last.then_inc(mixed, 1)

            def turn_x1(c, g):
                pe.wait_ge(x1_ready, 2 * (FIRST_GROUP[c] + g + 1))
                free_bank_t(("turn_x1", c, g))
                for j in range(TPG):
                    last = nc.tensor.transpose(ps_t[:, j * P:(j + 1) * P], x1[c % 3][:, g * TPG + j, :], ident[:])
                last.then_inc(turned, 1)

            def logits_of(c, g):
                n = FIRST_GROUP[c] + g
                pe.wait_ge(turn_copied, TURNS.index(("turn_x1", c, g)) + 1)
                if c >= 1 and g == 0:
                    pe.wait_ge(tokens_known, c)
                for j in range(TPG):
                    last = nc.tensor.matmul(ps_logits[:, g * TPG + j, :], x1_t[:, n % 2, j * P:(j + 1) * P],
                                            router_t[:], start=True, stop=True)
                last.then_inc(logits_done, 1)

            def rank(c, _):
                tiles, picks = TILES[c], picked[TILES[c]]
                pe.wait_ge(logits_read, c + 1)
                pe.wait_ge(picked_ready, c + 1)
                nc.tensor.matmul(ps_rank[:, 0:tiles + 1, :], before[:], picks[:], start=True, stop=False)
                for i in range(tiles):
                    rest = tiles - i
                    last = nc.tensor.matmul(ps_rank[:, i + 1:tiles + 1, :], ones[:],
                                            picks[:, i:i + 1, :].to_broadcast([P, rest, E]),
                                            start=False, stop=(i == tiles - 1))
                last.then_inc(rank_ready, 1)

            def hot_sums(c, q):
                if q == 0:
                    pe.wait_ge(rank_read, c + 1)
                for m in range(q * HOTS, (q + 1) * HOTS):
                    n = 2 * FIRST_GROUP[c] * TPG + m
                    pe.wait_ge(hot_ready, n + 1)
                    nc.tensor.matmul(ps_token[:, :, 0:BLOCKS[c]], lane_hot[:, n % HOT_RING, :],
                                     block_hot[:, n % HOT_RING, :, 0:BLOCKS[c]],
                                     start=(m == 0), stop=(m == 2 * TILES[c] - 1)).then_inc(hot_used, 1)

            def turn_weights(_, q):
                if q == 0:
                    pe.wait_ge(experts_in, 32)
                if q >= 2:
                    pe.wait_ge(w_t_ready, q - 1)
                for j in range(4):
                    m = 4 * q + j
                    raw = w1_raw[:, m, :] if m < 4 * E else w2_raw[:, m - 4 * E, :]
                    last = nc.tensor.transpose(w_bank(q)[:, j * P:(j + 1) * P], raw, ident[:])
                last.then_inc(w_turned, 1)

            def up(c, b, n):
                pe.wait_ge(xg_t_ready, min(n + 2, ALL_BLOCKS))
                if n + 2 > ALL_BLOCKS:
                    pe.wait_ge(w_up_ready, n + 1)
                for j in range(4):
                    last = nc.tensor.matmul(ps_h[n % 2][:, j * P:(j + 1) * P], w_up[:, n % 2, j * P:(j + 1) * P],
                                            xg_t[:, n % XT_RING, :], start=True, stop=True)
                last.then_inc(h_ready, 1)

            def turn_rows(c, b, n):
                if n < 2:
                    pe.wait_ge(w_t_ready, W_TURNS)
                elif n == 2:
                    pe.wait_ge(xg_t_ready, 1)
                pe.wait_ge(xg_ready[n % GATHER_RING], 16 * (n // GATHER_RING + 1))
                nc.tensor.transpose(ps_x[n % 2][:, 0:P], xg[n % GATHER_RING][:], ident[:]).then_inc(xg_turned, 1)

            def down(c, b, n):
                if b == 0:
                    pe.wait_ge(experts_known, c + 1)
                at = nc.values_load(w_at[c % 2][0:1, b:b + 1], engines=(PE,), min_val=0, max_val=(E - 1) * W_STRIDE,
                                    skip_runtime_bounds_check_because="the expert is capped at E - 1")
                if n >= 1:
                    pe.wait_ge(rows_ready, n)
                pe.wait_ge(y_ready, n + 1)
                for j in range(2):
                    last = nc.tensor.matmul(ps_u[:, 0:D], y[:, n % 2, j * P:(j + 1) * P],
                                            w_t[:, bass.ds(at + (2 * INTER + j * D), D)],
                                            start=(j == 0), stop=(j == 1))
                last.then_inc(u_ready, 1)

            for t in range(FIRST_TICK, END_TICK):
                run_blocks(t, ((0, turn_rows), (2, up), (3, down)))
                run_parts(t, {"turn_x": turn_x, "project": project, "mix": mix, "turn_x1": turn_x1,
                              "logits": logits_of, "rank": rank, "hot_sums": hot_sums,
                              "turn_weights": turn_weights})

        @block.scalar
        def _(act):
            act.wait_ge(w_ready, 16 * 5)
            nc.scalar.activation(lam[:], lam_log[:], ACT.Sigmoid).then_inc(lam_ready, 1)

            def squares(c, h):
                act.wait_ge(x_loaded[c], 16 * GROUPS[c])
                if c >= 1 and h == 0:
                    act.wait_ge(xn_ready, FIRST_GROUP[c - 1] + 1)
                for i in half_group(h):
                    last = nc.scalar.activation(square_junk[:, i, :], x_in[:, c % 2, i, :], ACT.Square,
                                                accum_out=sumsq[:, i:i + 1])
                last.then_inc(sumsq_ready, 1)

            def copy_xn(c, g):
                n = FIRST_GROUP[c] + g
                act.wait_ge(turned, TURNS.index(("turn_x", c, g)) + 1)
                if n >= 2:
                    act.wait_ge(proj_ready, 3 * (n - 1))
                nc.scalar.copy(x_norm_t[:, n % 2, :], ps_t[:]).then_inc(turn_copied, 1)

            def gates(c, g_k):
                g, k = g_k
                n = FIRST_GROUP[c] + g
                act.wait_ge(proj_ready, 3 * n + k + 1)
                if k < 2:
                    if n >= MAX_GROUPS:
                        act.wait_ge(state_ready, n - MAX_GROUPS + 1)
                    nc.scalar.activation((tanh_a, tanh_r)[k][:, n % MAX_GROUPS, :], project_bank(c, k)[:], ACT.Tanh,
                                         scale=0.5).then_inc(gates_ready, 1)
                else:
                    if n >= MAX_GROUPS:
                        act.wait_ge(state_ready, n - MAX_GROUPS + 1)
                    nc.scalar.copy(value[:, n % MAX_GROUPS, :], project_bank(c, k)[:]).then_inc(gates_ready, 1)

            def gelu(c, g):
                n = FIRST_GROUP[c] + g
                end = FIRST_GROUP[c] + min(g + GELU_GROUPS[c], GROUPS[c])
                act.wait_ge(gates_ready, 3 * end)
                while n < end:
                    place = n % MAX_GROUPS
                    count = min(end - n, MAX_GROUPS - place)
                    v = value[:, place:place + count, :].rearrange("p a b -> p (a b)")
                    nc.scalar.activation(v, v, ACT.Gelu).then_inc(gelu_ready, count)
                    n += count

            def copy_x1(c, g):
                n = FIRST_GROUP[c] + g
                act.wait_ge(turned, TURNS.index(("turn_x1", c, g)) + 1)
                if n >= 2:
                    act.wait_ge(logits_done, n - 1)
                nc.scalar.copy(x1_t[:, n % 2, :], ps_t[:]).then_inc(turn_copied, 1)

            def exps(c, _):
                tiles = TILES[c]
                act.wait_ge(shifted_ready, c + 1)
                nc.scalar.activation(exp_logits[c % 3][:, 0:tiles, :], shifted[c % 2][:, 0:tiles, :], ACT.Exp)
                nc.scalar.activation(exp_gap[c % 3][:, 0:tiles], top_gap[c % 2][:, 0:tiles], ACT.Exp
                                     ).then_inc(exps_ready, 1)

            def copy_weights(_, q):
                w_v = w_t[:].rearrange("p (e n) -> p e n", n=W_STRIDE)
                act.wait_ge(w_turned, q + 1)
                if q < E:
                    nc.scalar.copy(w_v[:, q, 0:2 * INTER], w_bank(q)[:]).then_inc(w_t_ready, 1)
                else:
                    m = 2 * (q - E)
                    nc.scalar.copy(w_v[:, m:m + 2, 2 * INTER:W_STRIDE],
                                   w_bank(q)[:].rearrange("p (e k) -> p e k", e=2)).then_inc(w_t_ready, 1)

            def copy_rows(c, b, n):
                act.wait_ge(xg_turned, n + 1)
                nc.scalar.copy(xg_t[:, n % XT_RING, :], ps_x[n % 2][:, 0:P]).then_inc(xg_t_ready, 1)

            def gate(c, b, n):
                act.wait_ge(h_ready, n + 1)
                nc.scalar.activation(silu[:, n % 2, :], ps_h[n % 2][:, 0:INTER], ACT.Silu).then_inc(silu_ready, 1)

            weights_at = {}

            def find_w(c, b, n):
                if b == 0:
                    act.wait_ge(experts_known, c + 1)
                weights_at[n] = nc.values_load(w_at[c % 2][0:1, b:b + 1], engines=(ACT_ENGINE,), min_val=0,
                                               max_val=(E - 1) * W_STRIDE,
                                               skip_runtime_bounds_check_because="the expert is capped at E - 1")

            def copy_w(c, b, n):
                if n == 0:
                    act.wait_ge(w_t_ready, W_TURNS)
                if n >= ROWS_RING + 2:
                    out_n = n - 2
                    act.wait_ge(rows_stored[out_n % ROWS_RING], 16 * (out_n // ROWS_RING))
                nc.scalar.copy(w_up[:, n % 2, :], w_t[:, bass.ds(weights_at.pop(n), 2 * INTER)]
                               ).then_inc(w_up_ready, 1)

            def copy_out(c, b, n):
                if n >= ALL_BLOCKS - 2:
                    act.wait_ge(rows_stored[n % ROWS_RING], 16 * (n // ROWS_RING))
                act.wait_ge(u_ready, n + 1)
                nc.scalar.copy(rows_out[:, n % ROWS_RING, :], ps_u[:, 0:D]).then_inc(rows_ready, 1)

            for t in range(FIRST_TICK, END_TICK):
                run_blocks(t, ((1, copy_w), (0, copy_rows), (0, find_w), (2, gate), (3, copy_out)))
                run_parts(t, {"squares": squares, "turn_x": copy_xn, "project": gates, "gelu": gelu,
                              "turn_x1": copy_x1, "exps": exps, "turn_weights": copy_weights})

        @block.vector
        def _(dve):
            steps = [0]

            def mark(ins):
                ins.then_inc(dve_step, 1)
                steps[0] += 1

            def after_marks():
                dve.wait_ge(dve_step, steps[0])

            def link(ins):
                mark(ins)
                after_marks()

            def root_seed(k, dst, src, eps, scale):
                half, whole = nr_half[k][:, 0:dst.shape[1]], nr_int[k][:, 0:dst.shape[1]]
                link(nc.vector.tensor_scalar(half, src, scale, eps, ALU.mult, ALU.add))
                link(nc.vector.tensor_scalar(whole, half.bitcast(I32), 1, None, ALU.arith_shift_right))
                mark(nc.vector.tensor_scalar(dst.bitcast(I32), whole, -1.0, RSQRT_MAGIC, ALU.mult, ALU.add))
                mark(nc.vector.tensor_scalar(half, half, -0.5, None, ALU.mult))

            def root_steps(k, dst, count):
                half, tmp = nr_half[k][:, 0:dst.shape[1]], nr_tmp[k][:, 0:dst.shape[1]]
                after_marks()
                for _ in range(count):
                    link(nc.vector.tensor_tensor(tmp, dst, dst, ALU.mult))
                    link(nc.vector.tensor_tensor(tmp, tmp, half, ALU.mult))
                    link(nc.vector.scalar_tensor_tensor(dst, tmp, 1.5, dst, ALU.add, ALU.mult))

            def variances(k, stats, rstd):
                tiles = rstd.shape[1]
                sum2, diff, v = mean[k][:, 0:tiles], mean_diff[k][:, 0:tiles], var[k][:, 0:tiles]
                after_marks()
                mark(nc.vector.tensor_tensor(sum2, stats[:, 0:tiles, 1], stats[:, 0:tiles, 4], ALU.add))
                mark(nc.vector.tensor_tensor(diff, stats[:, 0:tiles, 1], stats[:, 0:tiles, 4], ALU.subtract))
                mark(nc.vector.tensor_tensor(v, stats[:, 0:tiles, 2], stats[:, 0:tiles, 5], ALU.add))
                after_marks()
                link(nc.vector.tensor_tensor(diff, diff, diff, ALU.mult))
                link(nc.vector.scalar_tensor_tensor(v, diff, D / 4.0, v, ALU.mult, ALU.add))
                root_seed(k + 1, rstd, v, LN_EPS, 1.0 / D)

            def deviations(k, rstd, shift):
                root_steps(k + 1, rstd, 3)
                return nc.vector.scalar_tensor_tensor(shift, mean[k][:, 0:rstd.shape[1]], -0.5, rstd,
                                                      ALU.mult, ALU.mult)

            def rms(c, half):
                inv = rms_inv[:, 0:TILES[c]]
                if half == 0:
                    dve.wait_ge(sumsq_ready, 2 * FIRST_GROUP[c + 1])
                    if c >= 1:
                        dve.wait_ge(xn_ready, FIRST_GROUP[c])
                    root_seed(0, inv, sumsq[:, 0:TILES[c]], RMS_EPS, 1.0 / D)
                else:
                    root_steps(0, inv, 3)

            def normalise(c, g):
                n = FIRST_GROUP[c] + g
                if n >= 2:
                    dve.wait_ge(turned, TURNS.index(turn_of_x[n - 2]) + 1)
                tiles = slice(g * TPG, (g + 1) * TPG)
                nc.vector.tensor_tensor(x_norm[:, n % 2, :].rearrange("p (j d) -> p j d", j=TPG),
                                        x_in[:, c % 2, tiles, :],
                                        rms_inv[:, tiles].rearrange("p (j o) -> p j o", o=1).to_broadcast([P, TPG, D]),
                                        ALU.mult).then_inc(xn_ready, 1)

            def recur(c, g):
                n = FIRST_GROUP[c] + g
                dve.wait_ge(gelu_ready, n + 1)
                if n >= 1:
                    dve.wait_ge(state_ready, n)
                a = tanh_a[:, n % MAX_GROUPS, :]
                mark(nc.vector.tensor_scalar(gate_a[:], a, 0.5, 0.5, ALU.mult, ALU.add))
                mark(nc.vector.scalar_tensor_tensor(u1[:], a, -1.0, value[:, n % MAX_GROUPS, :], ALU.add, ALU.mult))

            def input_u(c, g):
                n = FIRST_GROUP[c] + g
                after_marks()
                mark(nc.vector.scalar_tensor_tensor(u2[:], tanh_r[:, n % MAX_GROUPS, :], 1.0, u1[:],
                                                    ALU.add, ALU.mult))

            def scan(c, g):
                n = FIRST_GROUP[c] + g
                after_marks()
                if n >= 2:
                    dve.wait_ge(mixed, n - 1)
                first = state[:, (n - 1) % 2, GROUP - 1:GROUP] if g % SEQ_GROUPS else 0.0
                nc.vector.tensor_tensor_scan(state[:, n % 2, :], gate_a[:], u2[:], first, ALU.mult, ALU.add
                                             ).then_inc(state_ready, 1)

            def residual(c, g):
                n = FIRST_GROUP[c] + g
                dve.wait_ge(mixed, n + 1)
                if c >= 1 and g == 0:
                    dve.wait_ge(x1_ready, 2 * FIRST_GROUP[c])
                tiles = slice(g * TPG, (g + 1) * TPG)
                nc.vector.scalar_tensor_tensor(z[:, tiles, :].rearrange("p j d -> p (j d)"),
                                               x_in[:, c % 2, tiles, :].rearrange("p j d -> p (j d)"), 2.0,
                                               ps_t[:], ALU.mult, ALU.add).then_inc(z_ready, 1)

            def z_bn_stats(c, g):
                dve.wait_ge(z_ready, FIRST_GROUP[c] + g + 1)
                for i in range(g * TPG, (g + 1) * TPG):
                    mark(nc.vector.bn_stats(stats[:, i, :], z[:, i, :]))

            def x1_statistics(c, half):
                tiles = TILES[c]
                if half == 0:
                    variances(0, stats, rstd[:, 0:tiles])
                else:
                    deviations(0, rstd[:, 0:tiles], neg_mean_rstd[:, 0:tiles]).then_inc(x1_stats, 1)

            def x1_of(c, h):
                if h == 0:
                    dve.wait_ge(x1_stats, c + 1)
                    if c >= 3:
                        dve.wait_ge(x1_stored[c - 3], 16 * GROUPS[c - 3])
                        dve.wait_ge(s_done, FIRST_GROUP[c - 2])
                for i in half_group(h):
                    last = nc.vector.tensor_scalar(x1[c % 3][:, i, :], z[:, i, :], rstd[:, i:i + 1],
                                                   neg_mean_rstd[:, i:i + 1], ALU.mult, ALU.add)
                last.then_inc(x1_ready, 1)

            def over_experts(v):
                return v.rearrange("p (i o) -> p i o", o=1).to_broadcast([P, v.shape[1], E])

            def pick_top(c, k, top):
                tiles = TILES[c]
                a, b, key = route_a[:, 0:tiles, :], route_b[:, 0:tiles], first_key[:, 0:tiles, :]
                link(nc.vector.tensor_reduce(top, logits[:, 0:tiles, :], AX.X, ALU.max))
                link(nc.vector.tensor_tensor(a, logits[:, 0:tiles, :], over_experts(top), ALU.is_equal))
                link(nc.vector.tensor_tensor(a, a, key, ALU.mult))
                link(nc.vector.tensor_reduce(b, a, AX.X, ALU.max))
                link(nc.vector.tensor_tensor(pick[:, k, 0:tiles, :], key, over_experts(b), ALU.is_equal))

            def pick_experts(c, k):
                tiles = TILES[c]
                values = logits[:, 0:tiles, :]
                if k == 0:
                    dve.wait_ge(logits_done, FIRST_GROUP[c + 1])
                    nc.vector.tensor_copy(values, ps_logits[:, 0:tiles, :]).then_inc(logits_read, 1)
                    dve.wait_ge(logits_read, c + 1)
                    pick_top(c, 0, top1[:, 0:tiles])
                    mark(nc.vector.tensor_tensor(shifted[c % 2][:, 0:tiles, :], values, over_experts(top1[:, 0:tiles]),
                                                 ALU.subtract))
                    after_marks()
                    link(nc.vector.scalar_tensor_tensor(values, pick[:, 0, 0:tiles, :], LOWEST, values,
                                                        ALU.mult, ALU.add))
                else:
                    pick_top(c, 1, top2[:, 0:tiles])
                    nc.vector.tensor_tensor(picked[tiles][:, 0:tiles, :], pick[:, 0, 0:tiles, :],
                                            pick[:, 1, 0:tiles, :], ALU.add).then_inc(picked_ready, 1)
                    nc.vector.tensor_tensor(top_gap[c % 2][:, 0:tiles], top2[:, 0:tiles], top1[:, 0:tiles],
                                            ALU.subtract).then_inc(shifted_ready, 1)

            def slots_of(c, half):
                tiles = TILES[c]
                base = route_a[:, 0:tiles, :]
                if half == 0:
                    dve.wait_ge(rank_ready, c + 1)
                    link(nc.vector.tensor_scalar(count_i[:], ps_rank[:, tiles, :], float(P - 1), None, ALU.add))
                    link(nc.vector.tensor_scalar(count_i[:], count_i[:], 7, None, ALU.arith_shift_right))
                    link(nc.vector.tensor_copy(blocks_of[:], count_i[:]))
                    link(nc.vector.tensor_tensor_scan(block_end[:], one_row[:], blocks_of[:], 0.0, ALU.mult, ALU.add))
                    link(nc.vector.tensor_tensor(slot_base[:], block_end[:], blocks_of[:], ALU.subtract))
                    link(nc.vector.tensor_scalar(slot_base[:], slot_base[:], float(P), None, ALU.mult))
                    nc.vector.tensor_tensor(base, ps_rank[:, 0:tiles, :],
                                            slot_base[:].rearrange("p (o e) -> p o e", o=1).to_broadcast([P, tiles, E]),
                                            ALU.add).then_inc(rank_read, 1)
                else:
                    dve.wait_ge(rank_read, c + 1)
                    for k in range(2):
                        mark(nc.vector.tensor_tensor(pick[:, k, 0:tiles, :], pick[:, k, 0:tiles, :], base, ALU.mult))
                    after_marks()
                    for k in range(2):
                        mark(nc.vector.tensor_reduce(slot_f[:, k, 0:tiles], pick[:, k, 0:tiles, :], AX.X, ALU.add))
                    after_marks()
                    slots = slot_i[c % 3][:, :, 0:tiles]
                    link(nc.vector.tensor_copy(slots, slot_f[:, :, 0:tiles]))
                    mark(nc.vector.tensor_scalar(part_i[:, 0, :, 0:tiles], slots, 7, None, ALU.arith_shift_right))
                    mark(nc.vector.tensor_scalar(part_i[:, 1, :, 0:tiles], slots, P - 1, None, ALU.bitwise_and))
                    after_marks()
                    mark(nc.vector.tensor_copy(slot_block[:, :, 0:tiles], part_i[:, 0, :, 0:tiles]))
                    mark(nc.vector.tensor_copy(slot_lane[:, :, 0:tiles], part_i[:, 1, :, 0:tiles]))

            def hots(c, q):
                if q == 0:
                    after_marks()
                for m in range(q * HOTS, (q + 1) * HOTS):
                    k, i = m // TILES[c], m % TILES[c]
                    n = 2 * FIRST_GROUP[c] * TPG + m
                    if n >= HOT_RING:
                        dve.wait_ge(hot_used, n - HOT_RING + 1)
                    nc.vector.tensor_scalar(lane_hot[:, n % HOT_RING, :], lane_iota[:], slot_lane[:, k, i:i + 1], None,
                                            ALU.is_equal)
                    nc.vector.scalar_tensor_tensor(block_hot[:, n % HOT_RING, :, 0:BLOCKS[c]],
                                                   block_iota[:, :, 0:BLOCKS[c]], slot_block[:, k, i:i + 1],
                                                   token_parts[:, i, :, 0:BLOCKS[c]], ALU.is_equal, ALU.mult
                                                   ).then_inc(hot_ready, 1)

            def block_experts(c, _):
                blocks = BLOCKS[c]
                link(nc.vector.tensor_tensor(ended[:, 0:blocks, :], block_no[:, 0:blocks, :],
                                             block_end[:].rearrange("p (o e) -> p o e", o=1)
                                             .to_broadcast([P, blocks, E]), ALU.is_ge))
                link(nc.vector.tensor_reduce(expert_f[:, 0:blocks], ended[:, 0:blocks, :], AX.X, ALU.add))
                link(nc.vector.tensor_scalar(expert_f[:, 0:blocks], expert_f[:, 0:blocks], float(E - 1), None, ALU.min))
                nc.vector.tensor_scalar(w_at[c % 2][:, 0:blocks], expert_f[:, 0:blocks], float(W_STRIDE), None,
                                        ALU.mult).then_inc(experts_known, 1)

            def token_lists(c, _):
                dve.wait_ge(hot_used, 2 * FIRST_GROUP[c + 1] * TPG)
                if c >= 2:
                    for place in range(GATHER_RING):
                        dve.wait_ge(xg_ready[place], 16 * fills(GATHER_RING, place, FIRST_BLOCK[c - 1]))
                blocks = BLOCKS[c]
                link(nc.vector.tensor_copy(token_at[:, :, 0:blocks], ps_token[:, :, 0:blocks]))
                mark(nc.vector.tensor_scalar(tile_parts[:, 0, 0:blocks], token_at[:, 1, 0:blocks], 2, None,
                                             ALU.arith_shift_right))
                mark(nc.vector.tensor_scalar(tile_parts[:, 1, 0:blocks], token_at[:, 1, 0:blocks], TPG - 1, None,
                                             ALU.bitwise_and))
                after_marks()
                link(nc.vector.scalar_tensor_tensor(token_pj[:, 0:blocks], token_at[:, 0, 0:blocks], float(TPG),
                                                    tile_parts[:, 1, 0:blocks], ALU.mult, ALU.add))
                nc.vector.scalar_tensor_tensor(token_of[c % 2][:, 0:blocks], tile_parts[:, 0, 0:blocks],
                                               float(GROUP), token_pj[:, 0:blocks], ALU.mult, ALU.add
                                               ).then_inc(tokens_known, 1)

            def product(c, b, n):
                dve.wait_ge(silu_ready, n + 1)
                nc.vector.tensor_tensor(y[:, n % 2, :], silu[:, n % 2, :], ps_h[n % 2][:, INTER:2 * INTER],
                                        ALU.mult).then_inc(y_ready, 1)

            def weights(c, _):
                tiles = TILES[c]
                dve.wait_ge(exps_ready, c + 1)
                link(nc.vector.tensor_reduce(exp_sum[:, 0:tiles], exp_logits[c % 3][:, 0:tiles, :], AX.X, ALU.add))
                link(nc.vector.reciprocal(weight[:, 0, 0:tiles], exp_sum[:, 0:tiles]))
                link(nc.vector.tensor_tensor(weight[:, 1, 0:tiles], weight[:, 0, 0:tiles], exp_gap[c % 3][:, 0:tiles],
                                             ALU.mult))

            def combine_first(c, g):
                dve.wait_ge(og_ready[g], og_fills(c + 1, g))
                if c >= 1 and g == 0:
                    dve.wait_ge(fin_ready, 2 * FIRST_GROUP[c])
                for i in range(g * TPG, (g + 1) * TPG):
                    mark(nc.vector.scalar_tensor_tensor(s[:, i, :], og[:, 0, i, :], weight[:, 0, i:i + 1],
                                                        x1[c % 3][:, i, :], ALU.mult, ALU.add))

            def combine_second(c, g):
                after_marks()
                for i in range(g * TPG, (g + 1) * TPG):
                    last = nc.vector.scalar_tensor_tensor(s[:, i, :], og[:, 1, i, :], weight[:, 1, i:i + 1],
                                                          s[:, i, :], ALU.mult, ALU.add)
                last.then_inc(s_done, 1)

            def out_bn_stats(c, g):
                dve.wait_ge(s_done, FIRST_GROUP[c] + g + 1)
                for i in range(g * TPG, (g + 1) * TPG):
                    mark(nc.vector.bn_stats(out_bn[:, i, :], s[:, i, :]))

            def out_statistics(c, half):
                tiles = TILES[c]
                if half == 0:
                    variances(1, out_bn, out_rstd[:, 0:tiles])
                else:
                    deviations(1, out_rstd[:, 0:tiles], out_shift[:, 0:tiles]).then_inc(out_stats, 1)

            def out_of(c, h):
                if h == 0:
                    dve.wait_ge(out_stats, c + 1)
                    if c >= 1:
                        dve.wait_ge(out_stored[c - 1], 16 * GROUPS[c - 1])
                for i in half_group(h):
                    last = nc.vector.tensor_scalar(fin[:, i, :], s[:, i, :], out_rstd[:, i:i + 1],
                                                   out_shift[:, i:i + 1], ALU.mult, ALU.add)
                last.then_inc(fin_ready, 1)

            turn_of_x = [part for part in TURNS if part[0] == "turn_x"]
            dve.wait_ge(w_ready, 16 * 5)
            dve.wait_ge(consts_ready, CONSTS)
            dve.wait_ge(lam_ready, 1)
            mark(nc.vector.tensor_scalar(w_in_sb[:], w_in_raw[:], w_norm_sb[:], None, ALU.mult))
            mark(nc.vector.tensor_scalar(w_out_sb[:], w_out_raw[:], lam[:], -0.25, ALU.mult, ALU.mult))
            after_marks()
            for t in range(FIRST_TICK, END_TICK):
                run_blocks(t, ((2, product),))
                run_parts(t, {"rms": rms, "normalise": normalise, "recur": recur, "input_u": input_u, "scan": scan, "z_bn": z_bn_stats,
                              "residual": residual, "x1_stats": x1_statistics, "x1": x1_of, "out": out_of, "pick": pick_experts,
                              "slots": slots_of, "block_experts": block_experts, "hots": hots,
                              "token_lists": token_lists, "weights": weights, "first": combine_first,
                              "second": combine_second, "out_bn": out_bn_stats, "out_stats": out_statistics})


_INS = ["L0_attn_x", "L0_attn_w_norm", "L0_attn_W_in", "L0_attn_lambda_log", "L0_attn_W_out",
        "L0_ffn_w1", "L0_ffn_w2", "L0_ffn_router_w"]


def kernel(**inputs):
    import numpy as _np
    import concourse.bacc as _bacc
    from concourse import mybir as _mybir
    from concourse.bass_utils import run_bass_kernel_spmd as _run

    nc = _bacc.Bacc("TRN2", target_bir_lowering=False, num_devices=1)
    arrays, args = {}, []
    for name in _INS:
        a = _np.ascontiguousarray(inputs[name])
        arrays[f"in_{name}"] = a
        args.append(nc.dram_tensor(f"in_{name}", a.shape, _mybir.dt.from_np(a.dtype), kind="ExternalInput").ap())
    out = nc.dram_tensor("out", (8, 1024, 128), _mybir.dt.from_np(_np.dtype("float32")), kind="ExternalOutput").ap()
    moe_layer(nc, *args, out)
    r = _run(nc, [arrays], core_ids=[0])
    return r.results[0]["out"]
```
